# Optimizing a Trainium2 kernel written in Bass

```python
import numpy as np
import jax
import jax.numpy as jnp

def _softmax(x, axis=-1):
    return jax.nn.softmax(x, axis=axis)

def _gelu(x):
    return jax.nn.gelu(x, approximate=True)

def _silu(x):
    return jax.nn.silu(x)

def _sigmoid(x):
    return jax.nn.sigmoid(x)

def _layernorm(x, axis=-1, eps=1e-05):
    m = jnp.mean(x, axis=axis, keepdims=True)
    v = jnp.var(x, axis=axis, keepdims=True)
    return (x - m) / jnp.sqrt(v + eps)

def _scatter_add(tgt, idx, src, axis=0):
    return tgt.at[idx].add(src)

def _segment_sum(src, seg, n):
    return jax.ops.segment_sum(src, seg, n)
kernel_name = 'mk_xattn_ffn_d1_seqx_r8_b540b8'

def setup_inputs(seed: int=0):
    np.random.seed(seed)
    _w = jnp.asarray

    def _rec_inputs():
        import jax
        import jax.numpy as jnp
        _rk = jax.random.key(seed)
        x = 7.22e-05 + 1 * jax.random.normal(jax.random.fold_in(_rk, 1), (2, 512, 128), jnp.float32)
        _lenS = 512 - jax.random.randint(jax.random.fold_in(_rk, 7), (2,), 0, max(1, 512 // 4) + 1, jnp.int32)
        _lenS2 = 32 - jax.random.randint(jax.random.fold_in(_rk, 8), (2,), 0, max(1, 32 // 4) + 1, jnp.int32)
        _ctx_1024P = jax.random.normal(jax.random.fold_in(_rk, 11), (2, 16, 128), jnp.float32)
        _ctx_1024c = jax.random.dirichlet(jax.random.fold_in(_rk, 511), 0.3 * jnp.ones((16,), jnp.float32), (2, 32))
        _ctx_1024t = jnp.einsum('bsk,bkd->bsd', _ctx_1024c, _ctx_1024P)
        _ctx_1024t = _ctx_1024t * jax.lax.rsqrt(jnp.mean(jnp.square(_ctx_1024t)) + 1e-12) * 0.953939
        ctx_1024 = 4.13588e-05 + 0.999923 * (_ctx_1024t + 0.3 * jax.random.normal(jax.random.fold_in(_rk, 611), (2, 32, 128), jnp.float32))
        return (x, ctx_1024)
    x, ctx_1024 = _rec_inputs()

    def _L0_xattn_setup():
        import jax, jax.numpy as jnp
        import numpy as np
        EMBED = 128
        HEADS = 16
        HEAD_DIM = EMBED // HEADS
        key = jax.random.key(seed)
        ks = jax.random.split(key, 10)
        B, N, M = (4, 256, 256)
        s = 1.0 / np.sqrt(EMBED)
        return {'xq': jax.random.normal(ks[0], (B, N, EMBED), jnp.float32), 'xk': jax.random.normal(ks[1], (B, M, EMBED), jnp.float32), 'xv': jax.random.normal(ks[2], (B, M, EMBED), jnp.float32), 'Wq': jax.random.normal(ks[3], (EMBED, EMBED), jnp.float32) * s, 'bq': jnp.zeros((EMBED,), jnp.float32), 'Wk': jax.random.normal(ks[4], (EMBED, EMBED), jnp.float32) * s, 'bk': jnp.zeros((EMBED,), jnp.float32), 'Wv': jax.random.normal(ks[5], (EMBED, EMBED), jnp.float32) * s, 'bv': jnp.zeros((EMBED,), jnp.float32), 'Wo': jax.random.normal(ks[6], (EMBED, EMBED), jnp.float32) * s}
    _L0_xattn_all = _L0_xattn_setup()
    _L0_xattn_in = {k: v for k, v in _L0_xattn_all.items() if k in ('Wq', 'bq', 'Wk', 'bk', 'Wv', 'bv', 'Wo')}
    del _L0_xattn_all

    def _L0_ffn_setup():
        import jax, jax.numpy as jnp
        import numpy as np
        ALPHA = 1.702
        LIMIT = 7.0
        EPS = 1e-05
        E = 16
        K = 4

        def _swiglu(h):
            x_glu = jnp.minimum(h[..., ::2], LIMIT)
            x_lin = jnp.clip(h[..., 1::2], LIMIT, LIMIT)
            return x_glu * jax.nn.sigmoid(ALPHA * x_glu) * (x_lin + 1.0)
        key = jax.random.key(seed)
        ks = jax.random.split(key, 7)
        B, T, H, I = (1, 256, 128, 128)
        x = jax.random.normal(ks[0], (B, T, H), jnp.float32)
        scale = jnp.ones((H,), jnp.float32)
        gate_w = jax.random.normal(ks[1], (E, H), jnp.float32) * 0.02
        gate_b = jnp.zeros((E,), jnp.float32)
        mlp1_w = jax.random.normal(ks[2], (E, 2 * I, H), jnp.float32) * 0.02
        mlp1_b = jax.random.normal(ks[3], (E, 2 * I), jnp.float32) * 0.02
        mlp2_w = jax.random.normal(ks[4], (E, H, I), jnp.float32) * 0.02
        mlp2_b = jax.random.normal(ks[5], (E, H), jnp.float32) * 0.02
        return dict(x=x, scale=scale, gate_w=gate_w, gate_b=gate_b, mlp1_w=mlp1_w, mlp1_b=mlp1_b, mlp2_w=mlp2_w, mlp2_b=mlp2_b)
    _L0_ffn_all = _L0_ffn_setup()
    _L0_ffn_in = {k: v for k, v in _L0_ffn_all.items() if k in ('scale', 'gate_w', 'gate_b', 'mlp1_w', 'mlp1_b', 'mlp2_w', 'mlp2_b')}
    del _L0_ffn_all
    return {'x': x, 'ctx_1024': ctx_1024, 'L0_xattn_Wq': _L0_xattn_in['Wq'], 'L0_xattn_bq': _L0_xattn_in['bq'], 'L0_xattn_Wk': _L0_xattn_in['Wk'], 'L0_xattn_bk': _L0_xattn_in['bk'], 'L0_xattn_Wv': _L0_xattn_in['Wv'], 'L0_xattn_bv': _L0_xattn_in['bv'], 'L0_xattn_Wo': _L0_xattn_in['Wo'], 'L0_ffn_scale': _L0_ffn_in['scale'], 'L0_ffn_gate_w': _L0_ffn_in['gate_w'], 'L0_ffn_gate_b': _L0_ffn_in['gate_b'], 'L0_ffn_mlp1_w': _L0_ffn_in['mlp1_w'], 'L0_ffn_mlp1_b': _L0_ffn_in['mlp1_b'], 'L0_ffn_mlp2_w': _L0_ffn_in['mlp2_w'], 'L0_ffn_mlp2_b': _L0_ffn_in['mlp2_b']}

def reference(x, ctx_1024, L0_xattn_Wq, L0_xattn_bq, L0_xattn_Wk, L0_xattn_bk, L0_xattn_Wv, L0_xattn_bv, L0_xattn_Wo, L0_ffn_scale, L0_ffn_gate_w, L0_ffn_gate_b, L0_ffn_mlp1_w, L0_ffn_mlp1_b, L0_ffn_mlp2_w, L0_ffn_mlp2_b):
    import jax
    import jax.numpy as jnp

    def _L0_xattn_ref(xq, xk, xv, Wq, bq, Wk, bk, Wv, bv, Wo):
        import jax, jax.numpy as jnp
        import numpy as np
        EMBED = 128
        HEADS = 16
        HEAD_DIM = EMBED // HEADS
        B, N, _ = xq.shape
        M = xk.shape[1]
        scale = HEAD_DIM ** (-0.5)
        q = (xq @ Wq.T + bq).reshape(B, N, HEADS, HEAD_DIM).transpose(0, 2, 1, 3)
        k = (xk @ Wk.T + bk).reshape(B, M, HEADS, HEAD_DIM).transpose(0, 2, 1, 3)
        v = (xv @ Wv.T + bv).reshape(B, M, HEADS, HEAD_DIM).transpose(0, 2, 1, 3)
        scores = jnp.einsum('bhnd,bhmd->bhnm', q, k) * scale
        weights = jax.nn.softmax(scores, axis=-1)
        out = jnp.einsum('bhnm,bhmd->bhnd', weights, v)
        out = out.transpose(0, 2, 1, 3).reshape(B, N, EMBED)
        return out @ Wo.T

    def _L0_ffn_ref(x, scale, gate_w, gate_b, mlp1_w, mlp1_b, mlp2_w, mlp2_b):
        import jax, jax.numpy as jnp
        import numpy as np
        ALPHA = 1.702
        LIMIT = 7.0
        EPS = 1e-05
        E = 16
        K = 4

        def _swiglu(h):
            x_glu = jnp.minimum(h[..., ::2], LIMIT)
            x_lin = jnp.clip(h[..., 1::2], LIMIT, LIMIT)
            return x_glu * jax.nn.sigmoid(ALPHA * x_glu) * (x_lin + 1.0)
        t = x * jax.lax.rsqrt(jnp.mean(x * x, axis=-1, keepdims=True) + EPS) * scale
        g = jnp.einsum('bth,eh->bte', t, gate_w) + gate_b
        vals, idx = jax.lax.top_k(g, K)
        w = jax.nn.softmax(vals, axis=-1)
        route = jnp.sum(jax.nn.one_hot(idx, E, dtype=t.dtype) * w[..., None], axis=-2)
        route_e = jnp.moveaxis(route, -1, 0)

        def step(acc, p):
            w1, b1, w2, b2, r = p
            h = jnp.einsum('bth,ih->bti', t, w1) + b1
            s = _swiglu(h)
            y = jnp.einsum('bti,hi->bth', s, w2) + b2
            return (acc + r[..., None] * y, None)
        acc, _ = jax.lax.scan(step, jnp.zeros_like(x), (mlp1_w, mlp1_b, mlp2_w, mlp2_b, route_e))
        return x + acc
    x = x + _L0_xattn_ref(_layernorm(x, axis=-1), ctx_1024, ctx_1024, L0_xattn_Wq, L0_xattn_bq, L0_xattn_Wk, L0_xattn_bk, L0_xattn_Wv, L0_xattn_bv, L0_xattn_Wo)
    x = x + _L0_ffn_ref(_layernorm(x, axis=-1), L0_ffn_scale, L0_ffn_gate_w, L0_ffn_gate_b, L0_ffn_mlp1_w, L0_ffn_mlp1_b, L0_ffn_mlp2_w, L0_ffn_mlp2_b)
    return x

_drawn_inputs = setup_inputs


def setup_inputs(seed=0):
    import zlib

    import numpy as np

    out = dict(_drawn_inputs(seed))
    spreads = {'L0_xattn_bq': (0.0, 0.309),
     'L0_xattn_bk': (0.0, 0.8),
     'L0_xattn_bv': (0.0, 0.1),
     'L0_ffn_scale': (1.0, 0.6),
     'L0_ffn_gate_b': (0.0, 0.1)}
    factors = {'L0_ffn_mlp1_b': 8.0, 'L0_ffn_mlp2_b': 8.0}
    for name, (base, spread) in spreads.items():
        noise = np.random.default_rng([zlib.crc32(name.encode()), seed]).standard_normal(out[name].shape)
        drawn = base * np.exp(spread * noise) if base else spread * noise
        out[name] = jnp.asarray(drawn.astype(out[name].dtype))
    for name, factor in factors.items():
        out[name] = (out[name] * factor).astype(out[name].dtype)
    return out
```

```python
from contextlib import ExitStack

import numpy as np

import concourse.bass as bass
from concourse import mybir

F32 = mybir.dt.float32
F32R = mybir.dt.float32r
BF16 = mybir.dt.bfloat16
I32 = mybir.dt.int32
U32 = mybir.dt.uint32
ALU = mybir.AluOpType
ACT = mybir.ActivationFunctionType
AX_X = mybir.AxisListType.X

P = 128
B = 2
S = 512
NT = S // P
M = 32
H = 16
HD = P // H
NC = H * M // P
HC = H // NC
VW = HC * HD + HC
E = 16
K = 4
EPS = 1e-5
ALPHA = 1.702
LIMIT = 7.0
SILU_LIMIT = float(ALPHA * LIMIT / (1.0 + np.exp(-ALPHA * LIMIT)))
ROUTE_SCALE = (LIMIT + 1.0) / ALPHA
SCORE_SCALE = float(HD) ** -0.5
STEPS = B * E
LAG = 3
NZ = 4
EG = 4

CTX0 = 0
WQ0 = CTX0 + B * M
WK0 = WQ0 + P
WV0 = WK0 + P
WO0 = WV0 + P
GW0 = WO0 + P
BQ0 = GW0 + E
BK0 = BQ0 + 1
SC0 = BK0 + 1
B10 = SC0 + 1
PACKED = B10 + E


def build_xattn_moe(nc, x, packed, bv, gate_b, w1, w2, b2, out):
    with ExitStack() as ctx:
        def sb(name, shape, dt):
            return ctx.enter_context(nc.sbuf_tensor(name, shape, dt))

        def bank(name):
            return ctx.enter_context(nc.psum_tensor(name, [P, 512], F32))

        def sem(name):
            return ctx.enter_context(nc.semaphore(name))

        ps_x = bank("ps_x")
        ps_q = bank("ps_q")
        ps_m = [bank("ps_m0"), bank("ps_m1")]
        ps_s = [bank("ps_s0"), bank("ps_s1")]
        ps_n = bank("ps_n")
        ps_d = bank("ps_d")
        ps_o = [ps_n, ps_d]
        ps_acc = [ps_d, ps_q]
        ps_gate = [ps_m[0], ps_n]
        ps_rt = [ps_m[1], ps_n]

        x_sb = sb("x_sb", [P, B * NT, P], F32)
        pk = sb("pk", [P, PACKED], F32)
        bv_row = sb("bv_row", [1, P], F32)
        gate_b_sb = sb("gate_b_sb", [P, E], F32)
        b2_sb = sb("b2_sb", [3 * E, P], F32)
        w1_sb = sb("w1_sb", [P, E * P], F32)
        w2_sb = sb("w2_sb", [P, E * P], F32)
        w1_hi = sb("w1_hi", [P, E * P], F32R)
        w1_lo = sb("w1_lo", [P, E * P], F32R)
        w2_hi = sb("w2_hi", [P, E * P], F32R)
        w2_lo = sb("w2_lo", [P, E * P], F32R)

        ident = sb("ident", [P, P], F32)
        ident_bf = sb("ident_bf", [P, P], BF16)
        ones_row = sb("ones_row", [1, P], F32)
        key_mask = sb("key_mask", [P, H], F32)
        val_mask = sb("val_mask", [P, HC], F32)
        neg_expand_f = sb("neg_expand_f", [H, H * M], F32)
        neg_expand = sb("neg_expand", [H, H * M], F32R)
        piece_eye = sb("piece_eye", [3 * E, E], BF16)
        pick = sb("pick", [3 * E, E, P], BF16)
        iota_e = sb("iota_e", [P, E], I32)
        neg_half = sb("neg_half", [P, NT], F32)

        wq_hi = sb("wq_hi", [P, P], F32R)
        wq_lo = sb("wq_lo", [P, P], F32R)
        gw_hi = sb("gw_hi", [P, E], F32R)
        gw_lo = sb("gw_lo", [P, E], F32R)
        b1_scaled = sb("b1_scaled", [P, E], F32)
        b2_scaled = sb("b2_scaled", [3 * E, P], F32)
        b2_rest = sb("b2_rest", [3 * E, 2, P], F32)
        b2_piece = sb("b2_piece", [3 * E, 3, P], BF16)

        ctx_rep = sb("ctx_rep", [P, B, HC, M], F32)
        kbd = sb("kbd", [P, B, H * M], F32)
        kbd_hi = sb("kbd_hi", [P, B, H * M], F32R)
        kbd_lo = sb("kbd_lo", [P, B, H * M], F32R)
        vbd = sb("vbd", [P, B, NC, VW], F32)

        stats = sb("stats", [P, 2 * B, NT, 6], F32)
        moments = sb("moments", [P, 2 * B, NT, 2], F32)
        spread = sb("spread", [P, 3 * B, NT], F32)
        rstd = sb("rstd", [P, 3 * B, NT], F32)
        xn = sb("xn", [P, B, NT, P], F32)
        xn_hi = sb("xn_hi", [P, B, S], F32R)
        xn_lo = sb("xn_lo", [P, B, S], F32R)
        q_hi = sb("q_hi", [P, B, S], F32R)
        q_lo = sb("q_lo", [P, B, S], F32R)
        row_max = sb("row_max", [P, B, NT, H], F32)
        max_t = sb("max_t", [H, B, S], F32R)
        probs = sb("probs", [P, B, NC, S], F32)
        rden = sb("rden", [P, B, 2, 2 * H], F32)
        attn = sb("attn", [P, B, NT, P], F32)
        attn_t = sb("attn_t", [P, B, S], F32)
        x1 = sb("x1", [P, B, NT, P], F32)
        xc = sb("xc", [P, B, NT, P], F32)
        ln = sb("ln", [P, B, NT, P], F32)
        x1_ln = sb("x1_ln", [P, B, NT, P], F32)
        t_hi = sb("t_hi", [P, B, S], F32R)
        t_lo = sb("t_lo", [P, B, S], F32R)

        gate = sb("gate", [P, B, NT, E], F32)
        top8 = sb("top8", [P, B, NT, 8], F32)
        top8_at = sb("top8_at", [P, B, NT, 8], U32)
        chosen4 = sb("chosen4", [P, B, NT, E, K], F32)
        chosen = sb("chosen", [P, B, NT, E], F32)
        gap = sb("gap", [P, B, NT, E], F32)
        gexp = sb("gexp", [P, B, NT, E], F32)
        gsel = sb("gsel", [P, B, NT, E], F32)
        gsum = sb("gsum", [P, B, NT], F32)
        grec = sb("grec", [P, B, NT], F32)
        route = sb("route", [P, B, 3, NT, E], F32)
        pieces = sb("pieces", [P, B, NT, 3, E], BF16)
        route_t = sb("route_t", [3 * E, B, S], BF16)

        act_f = sb("act_f", [P, 3, S], F32)
        z = sb("z", [P, 2, S], F32)
        z_hi = sb("z_hi", [P, NZ, S], F32R)
        z_lo = sb("z_lo", [P, NZ, S], F32R)
        acc_t = sb("acc_t", [P, B, S], F32)
        y = sb("y", [P, B, NT, P], F32)

        x_in = [sem(f"x_in{b}") for b in range(B)]
        packed_in = sem("packed_in")
        rows_in = sem("rows_in")
        w1_in = [sem(f"w1_in{h}") for h in range(2)]
        w2_in = [sem(f"w2_in{h}") for h in range(2)]
        out_done = sem("out_done")
        pool_step = sem("pool_step")
        dve_step = sem("dve_step")
        ident_ready = sem("ident_ready")
        masks_ready = sem("masks_ready")
        pick_ready = sem("pick_ready")
        rstd_ready = sem("rstd_ready")
        spread2_ready = sem("spread2_ready")
        rstd2_ready = sem("rstd2_ready")
        weights_split = sem("weights_split")
        small_ready = sem("small_ready")
        k_ready = sem("k_ready")
        v_ready = sem("v_ready")
        kbd_ready = sem("kbd_ready")
        vbd_ready = sem("vbd_ready")
        spread_ready = sem("spread_ready")
        xn_ready = sem("xn_ready")
        xnt_ready = sem("xnt_ready")
        xn_hi_ready = sem("xn_hi_ready")
        xn_split = sem("xn_split")
        q_ready = sem("q_ready")
        q_hi_ready = sem("q_hi_ready")
        q_split = sem("q_split")
        mscore_ready = sem("mscore_ready")
        max_done = sem("max_done")
        maxt_ready = sem("maxt_ready")
        max_t_ready = sem("max_t_ready")
        score_ready = sem("score_ready")
        exp_done = sem("exp_done")
        o_ready = sem("o_ready")
        attn_ready = sem("attn_ready")
        attnt_ready = sem("attnt_ready")
        attn_t_ready = sem("attn_t_ready")
        proj_ready = sem("proj_ready")
        x1_ready = sem("x1_ready")
        xc_ready = sem("xc_ready")
        ln_ready = sem("ln_ready")
        x1_ln_ready = sem("x1_ln_ready")
        tt_ready = sem("tt_ready")
        t_hi_ready = sem("t_hi_ready")
        t_split = sem("t_split")
        gate_ready = sem("gate_ready")
        gate_read = sem("gate_read")
        gap_ready = sem("gap_ready")
        gexp_ready = sem("gexp_ready")
        pieces_ready = sem("pieces_ready")
        routet_ready = sem("routet_ready")
        route_t_ready = sem("route_t_ready")
        h_ready = sem("h_ready")
        silu_done = sem("silu_done")
        rb_ready = sem("rb_ready")
        z_ready = sem("z_ready")
        z_hi_ready = sem("z_hi_ready")
        z_split = sem("z_split")
        mlp2_done = sem("mlp2_done")
        acc_t_ready = sem("acc_t_ready")
        yt_ready = sem("yt_ready")
        y_ready = sem("y_ready")

        x_tiles = x.rearrange("b (j p) d -> b p j d", p=P)
        out_tiles = out.rearrange("b (j p) d -> b p j d", p=P)
        half = E * P // 2

        def tile(t, b, j):
            return t[:, b, j * P:(j + 1) * P]

        def per_tile(v, n):
            return v.unsqueeze(2).to_broadcast([P, NT, n])

        block = ctx.enter_context(nc.Block())

        @block.sync
        def _(sp):
            sp.dma_start(x_sb[:, 0:NT, :], x_tiles[0]).then_inc(x_in[0], 16)
            sp.dma_start(x_sb[:, NT:, :], x_tiles[1]).then_inc(x_in[1], 16)
            for g in range(2):
                sp.dma_start(w1_sb[:, g * half:(g + 1) * half],
                             w1[0, :, g * half:(g + 1) * half]).then_inc(w1_in[g], 16)
                sp.dma_start(w2_sb[:, g * half:(g + 1) * half],
                             w2[:, g * half:(g + 1) * half]).then_inc(w2_in[g], 16)
            for b in range(B):
                sp.wait_ge(y_ready, b + 1)
                sp.dma_start(out_tiles[b], y[:, b]).then_inc(out_done, 16)
            sp.wait_ge(out_done, 16 * B)

        @block.gpsimd
        def _(pool):
            done = 0
            nc.gpsimd.memset(ident[:], 0.0).then_inc(pool_step, 1)
            nc.gpsimd.memset(key_mask[:], 1.0).then_inc(pool_step, 1)
            nc.gpsimd.memset(val_mask[:], 1.0).then_inc(pool_step, 1)
            nc.gpsimd.memset(neg_expand_f[:], -1.0).then_inc(pool_step, 1)
            nc.gpsimd.memset(piece_eye[:], 0.0).then_inc(pool_step, 1)
            nc.gpsimd.memset(neg_half[:], -0.5).then_inc(pool_step, 1)
            done += 6
            pool.wait_ge(pool_step, done)
            nc.gpsimd.affine_select(out=ident[:], in_=ident[:], compare_op=ALU.not_equal, fill=1.0,
                                    base=0, pattern=[[-1, P]], channel_multiplier=1).then_inc(ident_ready, 1)
            nc.gpsimd.affine_select(out=key_mask[:], in_=key_mask[:], compare_op=ALU.is_ge, fill=0.0,
                                    base=0, pattern=[[-HD, H]], channel_multiplier=1).then_inc(pool_step, 1)
            nc.gpsimd.affine_select(out=val_mask[:], in_=val_mask[:], compare_op=ALU.is_ge, fill=0.0,
                                    base=0, pattern=[[-M, HC]], channel_multiplier=1).then_inc(pool_step, 1)
            done += 2
            pool.wait_ge(pool_step, done)
            nc.gpsimd.affine_select(out=key_mask[:], in_=key_mask[:], compare_op=ALU.is_ge, fill=0.0,
                                    base=HD - 1, pattern=[[HD, H]], channel_multiplier=-1).then_inc(masks_ready, 1)
            nc.gpsimd.affine_select(out=val_mask[:], in_=val_mask[:], compare_op=ALU.is_ge, fill=0.0,
                                    base=M - 1, pattern=[[M, HC]], channel_multiplier=-1).then_inc(masks_ready, 1)

            def inverse_root(n):
                pool.wait_ge(spread_ready, n + 1)
                nc.gpsimd.tensor_tensor(rstd[:, n], spread[:, n], neg_half[:], ALU.pow).then_inc(rstd_ready, 1)

            inverse_root(0)
            inverse_root(1)
            nc.gpsimd.affine_select(out=neg_expand_f[:], in_=neg_expand_f[:], compare_op=ALU.is_equal, fill=0.0,
                                    base=0, pattern=[[-1, H], [0, M]], channel_multiplier=1).then_inc(masks_ready, 1)
            for k in range(3):
                if k:
                    pool.wait_ge(pool_step, done)
                nc.gpsimd.affine_select(out=piece_eye[:], in_=piece_eye[:], compare_op=ALU.not_equal, fill=1.0,
                                        base=-E * k, pattern=[[-1, E]], channel_multiplier=1).then_inc(pool_step, 1)
                done += 1
            nc.gpsimd.iota(iota_e[:], pattern=[[1, E]], base=0, channel_multiplier=0).then_inc(pick_ready, 1)
            pool.wait_ge(pool_step, done)
            nc.gpsimd.tensor_copy(pick[:], piece_eye[:].unsqueeze(2).to_broadcast([3 * E, E, P])).then_inc(pick_ready, 1)

            def split_weights(g, w, hi, lo, arrived):
                cols = slice(g * EG * P, (g + 1) * EG * P)
                pool.wait_ge(arrived[g * EG * P // half], 16)
                nc.gpsimd.tensor_copy(hi[:, cols], w[:, cols]).then_inc(pool_step, 1)
                nonlocal done
                done += 1
                pool.wait_ge(pool_step, done)
                nc.gpsimd.tensor_tensor(lo[:, cols], w[:, cols], hi[:, cols].bitcast(F32),
                                        ALU.subtract).then_inc(weights_split, 1)

            split_weights(0, w1_sb, w1_hi, w1_lo, w1_in)
            split_weights(0, w2_sb, w2_hi, w2_lo, w2_in)
            inverse_root(2)
            split_weights(1, w1_sb, w1_hi, w1_lo, w1_in)
            inverse_root(3)
            split_weights(1, w2_sb, w2_hi, w2_lo, w2_in)
            for b in range(B):
                pool.wait_ge(spread2_ready, b + 1)
                nc.gpsimd.tensor_tensor(rstd[:, 2 * B + b], spread[:, 2 * B + b], neg_half[:],
                                        ALU.pow).then_inc(rstd2_ready, 1)
            for g in range(2, E // EG):
                split_weights(g, w1_sb, w1_hi, w1_lo, w1_in)
                split_weights(g, w2_sb, w2_hi, w2_lo, w2_in)
            for b in range(B):
                pool.wait_ge(ln_ready, b + 1)
                nc.gpsimd.tensor_tensor(x1_ln[:, b], x1[:, b], ln[:, b], ALU.add).then_inc(x1_ln_ready, 1)

        @block.tensor
        def _(pe):
            mm, tr = nc.tensor.matmul, nc.tensor.transpose

            def split_product(acc, lhs_hi, lhs_lo, rhs_hi, rhs_lo, start=True, stop=True):
                mm(acc, lhs_hi, rhs_hi, start=start, stop=False)
                mm(acc, lhs_hi, rhs_lo, start=False, stop=False)
                return mm(acc, lhs_lo, rhs_hi, start=False, stop=stop)

            def project_context():
                pe.wait_ge(packed_in, 16)
                mm(ps_n[:, 0:B * M], pk[:, WK0:WK0 + P], pk[:, CTX0:CTX0 + B * M],
                   start=True, stop=True).then_inc(k_ready, 1)
                pe.wait_ge(rows_in, 16 * 5)
                pe.wait_ge(small_ready, 1)
                for b in range(B):
                    v_ps = ps_d[:, b * P:(b + 1) * P]
                    mm(v_ps, ctx_rep[:, b].rearrange("p a m -> p (a m)"), pk[:, WV0:WV0 + P], start=True, stop=False)
                    last = mm(v_ps, ones_row[:], bv_row[:], start=False, stop=True)
                last.then_inc(v_ready, 1)

            def transpose_xn(b):
                if b:
                    pe.wait_ge(xn_split, b)
                else:
                    pe.wait_ge(ident_ready, 1)
                pe.wait_ge(xn_ready, b + 1)
                for j in range(NT):
                    last = tr(ps_x[:, j * P:(j + 1) * P], xn[:, b, j], ident[:])
                last.then_inc(xnt_ready, 1)

            def project_q(b):
                pe.wait_ge(xn_split, b + 1)
                if b:
                    pe.wait_ge(q_split, b)
                else:
                    pe.wait_ge(small_ready, 2)
                split_product(ps_q[:], wq_hi[:], wq_lo[:], xn_hi[:, b], xn_lo[:, b]).then_inc(q_ready, 1)

            def max_scores(b, j):
                n = b * NT + j
                if j == 0:
                    pe.wait_ge(q_split, b + 1)
                    pe.wait_ge(kbd_ready, b + 1)
                if n >= 2:
                    pe.wait_ge(max_done, n - 1)
                mm(ps_m[n % 2][:], tile(q_hi, b, j), kbd_hi[:, b], start=True, stop=True).then_inc(mscore_ready, 1)

            def transpose_max(b):
                pe.wait_ge(max_done, NT * (b + 1))
                pe.wait_ge(xn_split, B)
                if b:
                    pe.wait_ge(max_t_ready, b)
                for j in range(NT):
                    last = tr(ps_x[0:H, j * P:(j + 1) * P], row_max[:, b, j], ident[:])
                last.then_inc(maxt_ready, 1)

            def scores(b, c):
                n = b * NC + c
                cols = slice(c * P, (c + 1) * P)
                if c == 0:
                    pe.wait_ge(max_t_ready, b + 1)
                    pe.wait_ge(small_ready, 3)
                if n >= 2:
                    pe.wait_ge(exp_done, n - 1)
                split_product(ps_s[n % 2][:], kbd_hi[:, b, cols], kbd_lo[:, b, cols], q_hi[:, b], q_lo[:, b], stop=False)
                mm(ps_s[n % 2][:], neg_expand[:, cols], max_t[:, b], start=False, stop=True).then_inc(score_ready, 1)

            def weigh_values(b):
                pe.wait_ge(exp_done, NC * (b + 1))
                pe.wait_ge(vbd_ready, B)
                if b:
                    pe.wait_ge(attn_ready, 2 * b)
                for j in range(NT):
                    for c in range(NC):
                        at = (j % 2) * NC * VW + c * VW
                        last = mm(ps_o[j // 2][:, at:at + VW], probs[:, b, c, j * P:(j + 1) * P], vbd[:, b, c],
                                  start=True, stop=True)
                    if j % 2:
                        last.then_inc(o_ready, 1)

            def transpose_attn(b):
                pe.wait_ge(attn_ready, 2 * (b + 1))
                pe.wait_ge(max_t_ready, B)
                if b:
                    pe.wait_ge(t_split, b)
                for j in range(NT):
                    last = tr(ps_x[:, j * P:(j + 1) * P], attn[:, b, j], ident[:])
                last.then_inc(attnt_ready, 1)

            def project_out(b):
                pe.wait_ge(attn_t_ready, b + 1)
                pe.wait_ge(q_split, B)
                if b:
                    pe.wait_ge(x1_ready, b)
                for j in range(NT):
                    last = mm(ps_q[:, j * P:(j + 1) * P], tile(attn_t, b, j), pk[:, WO0:WO0 + P], start=True, stop=True)
                last.then_inc(proj_ready, 1)

            def transpose_t(b):
                pe.wait_ge(xc_ready, b + 1)
                pe.wait_ge(attn_t_ready, b + 1)
                for j in range(NT):
                    last = tr(ps_x[:, j * P:(j + 1) * P], xc[:, b, j], ident[:])
                last.then_inc(tt_ready, 1)

            def gate_logits(b):
                pe.wait_ge(t_split, b + 1)
                pe.wait_ge(max_done, B * NT)
                pe.wait_ge(attn_ready, 2 * (b + 1))
                for j in range(NT):
                    g = ps_gate[b][:, j * E:(j + 1) * E]
                    split_product(g, tile(t_hi, b, j), tile(t_lo, b, j), gw_hi[:], gw_lo[:], stop=False)
                    last = mm(g, tile(t_lo, b, j), gw_lo[:], start=False, stop=True)
                last.then_inc(gate_ready, 1)

            def transpose_route(b):
                pe.wait_ge(pieces_ready, b + 1)
                pe.wait_ge(gate_read, b + 1)
                pe.wait_ge(small_ready, 4)
                rt = ps_rt[b][:].bitcast(BF16)
                for j in range(NT):
                    last = tr(rt[0:3 * E, j * P:(j + 1) * P], pieces[:, b, j].rearrange("p k e -> p (k e)"), ident_bf[:])
                last.then_inc(routet_ready, 1)

            def mlp1(s):
                b, e = divmod(s, E)
                cols = slice(e * P, (e + 1) * P)
                if e == 0:
                    pe.wait_ge(t_split, b + 1)
                if b == 0 and e % EG == 0:
                    pe.wait_ge(weights_split, 2 * (e // EG) + 1)
                if s >= 2:
                    pe.wait_ge(silu_done, s - 1)
                split_product(ps_s[s % 2][:], w1_hi[:, cols], w1_lo[:, cols], t_hi[:, b], t_lo[:, b]).then_inc(h_ready, 1)

            def spread_route(s):
                b, e = divmod(s, E)
                if e == 0:
                    pe.wait_ge(route_t_ready, b + 1)
                    pe.wait_ge(pick_ready, 2)
                if s >= 2:
                    pe.wait_ge(z_ready, s - 1)
                mm(ps_m[s % 2][:], pick[:, e], route_t[:, b], start=True, stop=True).then_inc(rb_ready, 1)

            def mlp2(s):
                b, e = divmod(s, E)
                cols = slice(e * P, (e + 1) * P)
                if e == 0:
                    pe.wait_ge(small_ready, 5)
                    for k in range(3):
                        mm(ps_acc[b][:], b2_piece[:, k], route_t[:, b], start=(k == 0), stop=False)
                if b == 0 and e % EG == 0:
                    pe.wait_ge(weights_split, 2 * (e // EG) + 2)
                pe.wait_ge(z_split, s + 1)
                split_product(ps_acc[b][:], w2_hi[:, cols], w2_lo[:, cols], z_hi[:, s % NZ], z_lo[:, s % NZ],
                              start=False, stop=(e == E - 1)).then_inc(mlp2_done, 1)

            def transpose_y(b):
                pe.wait_ge(acc_t_ready, b + 1)
                pe.wait_ge(t_split, B)
                if b:
                    pe.wait_ge(y_ready, b)
                for j in range(NT):
                    last = tr(ps_x[:, j * P:(j + 1) * P], tile(acc_t, b, j), ident[:])
                last.then_inc(yt_ready, 1)

            project_context()
            transpose_xn(0)
            project_q(0)
            transpose_xn(1)
            for j in range(NT):
                max_scores(0, j)
            project_q(1)
            transpose_max(0)
            for c in range(NC):
                scores(0, c)
                max_scores(1, c)
            transpose_max(1)
            weigh_values(0)
            scores(1, 0)
            scores(1, 1)
            transpose_attn(0)
            scores(1, 2)
            scores(1, 3)
            project_out(0)
            weigh_values(1)
            transpose_t(0)
            gate_logits(0)
            transpose_attn(1)
            project_out(1)
            mlp1(0)
            mlp1(1)
            transpose_route(0)
            spread_route(0)
            spread_route(1)
            for s in range(2, STEPS + LAG):
                if s < STEPS:
                    mlp1(s)
                    spread_route(s)
                if s == 2:
                    transpose_t(1)
                    gate_logits(1)
                if s == 6:
                    transpose_route(1)
                if s >= LAG:
                    mlp2(s - LAG)
                if s == E + LAG + 1:
                    transpose_y(0)
            transpose_y(1)

        @block.scalar
        def _(act):
            act.dma_start(pk[:], packed).then_inc(packed_in, 16)
            act.dma_start(bv_row[:], bv).then_inc(rows_in, 16)
            act.dma_start(gate_b_sb[:], gate_b.to_broadcast([P, E])).then_inc(rows_in, 16)
            for k in range(3):
                act.dma_start(b2_sb[k * E:(k + 1) * E, :], b2).then_inc(rows_in, 16)

            def xn_high(b):
                act.wait_ge(xnt_ready, b + 1)
                nc.scalar.activation(xn_hi[:, b], ps_x[:], ACT.Copy).then_inc(xn_hi_ready, 1)

            def q_high(b):
                act.wait_ge(q_ready, b + 1)
                nc.scalar.activation(q_hi[:, b], ps_q[:], ACT.Identity, bias=pk[:, BQ0:BQ0 + 1]).then_inc(q_hi_ready, 1)

            def max_rows(b):
                act.wait_ge(maxt_ready, b + 1)
                nc.scalar.activation(max_t[:, b], ps_x[0:H, :], ACT.Copy).then_inc(max_t_ready, 1)

            def exponent(b, c):
                n = b * NC + c
                act.wait_ge(score_ready, n + 1)
                nc.scalar.activation(probs[:, b, c], ps_s[n % 2][:], ACT.Exp, scale=SCORE_SCALE).then_inc(exp_done, 1)

            def attn_copy(b):
                act.wait_ge(attnt_ready, b + 1)
                nc.scalar.activation(attn_t[:, b], ps_x[:], ACT.Copy).then_inc(attn_t_ready, 1)

            def t_high(b):
                act.wait_ge(tt_ready, b + 1)
                nc.scalar.activation(t_hi[:, b], ps_x[:], ACT.Copy, scale=pk[:, SC0:SC0 + 1]).then_inc(t_hi_ready, 1)

            def gate_exp(b):
                act.wait_ge(gap_ready, b + 1)
                nc.scalar.activation(gexp[:, b], gap[:, b], ACT.Exp).then_inc(gexp_ready, 1)

            def silu(s):
                e = s % E
                act.wait_ge(h_ready, s + 1)
                if s >= 3:
                    act.wait_ge(z_ready, s - 2)
                nc.scalar.activation(act_f[:, s % 3], ps_s[s % 2][:], ACT.Silu, scale=ALPHA,
                                     bias=b1_scaled[:, e:e + 1]).then_inc(silu_done, 1)

            def z_high(s):
                act.wait_ge(z_ready, s + 1)
                if s >= NZ:
                    act.wait_ge(mlp2_done, s - NZ + 1)
                nc.scalar.activation(z_hi[:, s % NZ], z[:, s % 2], ACT.Copy).then_inc(z_hi_ready, 1)

            def acc_copy(b):
                act.wait_ge(mlp2_done, E * (b + 1))
                nc.scalar.activation(acc_t[:, b], ps_acc[b][:], ACT.Copy).then_inc(acc_t_ready, 1)

            xn_high(0)
            q_high(0)
            xn_high(1)
            q_high(1)
            max_rows(0)
            for c in range(NC):
                exponent(0, c)
            max_rows(1)
            exponent(1, 0)
            exponent(1, 1)
            attn_copy(0)
            exponent(1, 2)
            exponent(1, 3)
            t_high(0)
            attn_copy(1)
            gate_exp(0)
            act.wait_ge(small_ready, 6)
            silu(0)
            silu(1)
            for s in range(2, STEPS + 1):
                z_high(s - 2)
                if s == 3:
                    t_high(1)
                if s == 5:
                    gate_exp(1)
                if s == E + LAG:
                    acc_copy(0)
                if s < STEPS:
                    silu(s)
            z_high(STEPS - 1)
            acc_copy(1)

        @block.vector
        def _(dve):
            steps = [0]

            def step(instruction):
                steps[0] += 1
                instruction.then_inc(dve_step, 1)
                return steps[0]

            def normalise(n, src, dst, finish):
                for j in range(NT):
                    at = step(nc.vector.bn_stats(stats[:, n, j], src(j)))
                dve.wait_ge(dve_step, at)
                for j in range(NT):
                    at = step(nc.vector.bn_aggr(moments[:, n, j], stats[:, n, j]))
                dve.wait_ge(dve_step, at)
                finish().then_inc(spread_ready, 1)

            def apply_norm(n, src, dst, ready):
                dve.wait_ge(rstd_ready, n + 1)
                for j in range(NT):
                    last = nc.vector.tensor_scalar(dst(j), src(j), moments[:, n, j, 0:1], rstd[:, n, j:j + 1],
                                                   ALU.subtract, ALU.mult)
                last.then_inc(ready, 1)

            def norm1(b):
                dve.wait_ge(x_in[b], 16)
                normalise(b, lambda j: x_sb[:, b * NT + j], None,
                          lambda: nc.vector.tensor_scalar(spread[:, b], moments[:, b, :, 1], EPS, None, ALU.add))

            def apply1(b):
                apply_norm(b, lambda j: x_sb[:, b * NT + j], lambda j: xn[:, b, j], xn_ready)

            def xn_low(b):
                dve.wait_ge(xn_hi_ready, b + 1)
                nc.vector.tensor_tensor(xn_lo[:, b], ps_x[:], xn_hi[:, b].bitcast(F32), ALU.subtract).then_inc(xn_split, 1)

            def q_low(b):
                dve.wait_ge(q_hi_ready, b + 1)
                nc.vector.scalar_tensor_tensor(out=q_lo[:, b], in0=ps_q[:], scalar=pk[:, BQ0:BQ0 + 1],
                                               in1=q_hi[:, b].bitcast(F32), op0=ALU.add, op1=ALU.subtract).then_inc(q_split, 1)

            def small_operands():
                dve.wait_ge(packed_in, 16)
                nc.vector.memset(ones_row[:], 1.0).then_inc(dve_step, 1)
                steps[0] += 1
                nc.vector.tensor_copy(ctx_rep[:], pk[:, CTX0:CTX0 + B * M].rearrange("p (b m) -> p b m", b=B)
                                      .unsqueeze(2).to_broadcast([P, B, HC, M])).then_inc(small_ready, 1)
                at = step(nc.vector.tensor_copy(wq_hi[:], pk[:, WQ0:WQ0 + P]))
                step(nc.vector.tensor_copy(gw_hi[:], pk[:, GW0:GW0 + E]))
                at += 1
                dve.wait_ge(dve_step, at)
                step(nc.vector.tensor_tensor(gw_lo[:], pk[:, GW0:GW0 + E], gw_hi[:].bitcast(F32), ALU.subtract))
                nc.vector.tensor_tensor(wq_lo[:], pk[:, WQ0:WQ0 + P], wq_hi[:].bitcast(F32), ALU.subtract).then_inc(small_ready, 1)

            def key_blocks():
                dve.wait_ge(k_ready, 1)
                dve.wait_ge(masks_ready, 2)
                for b in range(B):
                    at = step(nc.vector.scalar_tensor_tensor(
                        out=kbd[:, b].rearrange("p (h m) -> p h m", h=H),
                        in0=ps_n[:, b * M:(b + 1) * M].unsqueeze(1).to_broadcast([P, H, M]),
                        scalar=pk[:, BK0:BK0 + 1], in1=key_mask[:].unsqueeze(2).to_broadcast([P, H, M]),
                        op0=ALU.add, op1=ALU.mult))
                    dve.wait_ge(dve_step, at)
                    at = step(nc.vector.tensor_copy(kbd_hi[:, b], kbd[:, b]))
                    dve.wait_ge(dve_step, at)
                    nc.vector.tensor_tensor(kbd_lo[:, b], kbd[:, b], kbd_hi[:, b].bitcast(F32), ALU.subtract).then_inc(kbd_ready, 1)

            def value_blocks():
                dve.wait_ge(v_ready, 1)
                for b in range(B):
                    nc.vector.tensor_tensor(
                        vbd[:, b, :, 0:HC * HD].rearrange("p c (a d) -> p c a d", a=HC),
                        ps_d[:, b * P:(b + 1) * P].rearrange("p (c a d) -> p c a d", c=NC, a=HC),
                        val_mask[:].unsqueeze(1).unsqueeze(3).to_broadcast([P, NC, HC, HD]), ALU.mult).then_inc(dve_step, 1)
                    steps[0] += 1
                    nc.vector.tensor_copy(vbd[:, b, :, HC * HD:VW],
                                          val_mask[:].unsqueeze(1).to_broadcast([P, NC, HC])).then_inc(vbd_ready, 1)

            def route_operands():
                dve.wait_ge(masks_ready, 3)
                nc.vector.tensor_copy(neg_expand[:], neg_expand_f[:]).then_inc(small_ready, 1)
                dve.wait_ge(ident_ready, 1)
                nc.vector.tensor_copy(ident_bf[:], ident[:]).then_inc(small_ready, 1)

            def bias_operands():
                dve.wait_ge(rows_in, 16 * 5)
                at = step(nc.vector.tensor_scalar(b2_scaled[:], b2_sb[:], 1.0 / ROUTE_SCALE, None, ALU.mult))
                rest = b2_scaled[:]
                for k in range(2):
                    dve.wait_ge(dve_step, at)
                    at = step(nc.vector.tensor_copy(b2_piece[:, k], rest))
                    dve.wait_ge(dve_step, at)
                    at = step(nc.vector.tensor_tensor(b2_rest[:, k], rest, b2_piece[:, k], ALU.subtract))
                    rest = b2_rest[:, k]
                dve.wait_ge(dve_step, at)
                nc.vector.tensor_copy(b2_piece[:, 2], rest).then_inc(small_ready, 1)
                nc.vector.tensor_scalar(b1_scaled[:], pk[:, B10:B10 + E], ALPHA, None, ALU.mult).then_inc(small_ready, 1)

            def maximum(b, j):
                n = b * NT + j
                dve.wait_ge(mscore_ready, n + 1)
                nc.vector.tensor_reduce(row_max[:, b, j], ps_m[n % 2][:].rearrange("p (h m) -> p h m", h=H),
                                        AX_X, ALU.max).then_inc(max_done, 1)

            def divide(b):
                for i in range(2):
                    dve.wait_ge(o_ready, 2 * b + i + 1)
                    o = ps_o[i][:, 0:2 * NC * VW].rearrange("p (c w) -> p c w", w=VW)
                    r = rden[:, b, i].rearrange("p (c a) -> p c a", a=HC)
                    at = step(nc.vector.reciprocal(r, o[:, :, HC * HD:VW]))
                    dve.wait_ge(dve_step, at)
                    nc.vector.tensor_tensor(
                        attn[:, b, 2 * i:2 * i + 2].rearrange("p j (c a d) -> p (j c) a d", c=NC, a=HC),
                        o[:, :, 0:HC * HD].rearrange("p c (a d) -> p c a d", a=HC),
                        r.unsqueeze(3).to_broadcast([P, 2 * NC, HC, HD]), ALU.mult).then_inc(attn_ready, 1)

            def residual1(b):
                dve.wait_ge(proj_ready, b + 1)
                nc.vector.tensor_tensor(x1[:, b].rearrange("p j d -> p (j d)"), ps_q[:],
                                        x_sb[:, b * NT:(b + 1) * NT].rearrange("p j d -> p (j d)"), ALU.add).then_inc(x1_ready, 1)
                dve.wait_ge(x1_ready, b + 1)

            def norm2(b):
                n = B + b
                normalise(n, lambda j: x1[:, b, j], None,
                          lambda: nc.vector.tensor_scalar(spread[:, n], moments[:, n, :, 1], 1.0 + EPS, EPS * EPS,
                                                          ALU.mult, ALU.add))
                nc.vector.tensor_scalar(spread[:, B + n], moments[:, n, :, 1], EPS, None, ALU.add).then_inc(spread2_ready, 1)

            def apply2(b):
                apply_norm(B + b, lambda j: x1[:, b, j], lambda j: xc[:, b, j], xc_ready)

            def norm_x1(b):
                dve.wait_ge(rstd2_ready, b + 1)
                for j in range(NT):
                    last = nc.vector.tensor_scalar(ln[:, b, j], x1[:, b, j], moments[:, B + b, j, 0:1],
                                                   rstd[:, 2 * B + b, j:j + 1], ALU.subtract, ALU.mult)
                last.then_inc(ln_ready, 1)

            def t_low(b):
                dve.wait_ge(t_hi_ready, b + 1)
                nc.vector.scalar_tensor_tensor(out=t_lo[:, b], in0=ps_x[:], scalar=pk[:, SC0:SC0 + 1],
                                               in1=t_hi[:, b].bitcast(F32), op0=ALU.mult, op1=ALU.subtract).then_inc(t_split, 1)

            def choose(b):
                dve.wait_ge(gate_ready, b + 1)
                dve.wait_ge(rows_in, 16 * 5)
                nc.vector.tensor_tensor(gate[:, b], ps_gate[b][:, 0:NT * E].rearrange("p (j e) -> p j e", e=E),
                                        gate_b_sb[:].unsqueeze(1).to_broadcast([P, NT, E]), ALU.add).then_inc(gate_read, 1)
                dve.wait_ge(gate_read, b + 1)
                for j in range(NT):
                    at = step(nc.vector.max(top8[:, b, j], gate[:, b, j]))
                dve.wait_ge(dve_step, at)
                nc.vector.tensor_tensor(gap[:, b], gate[:, b], top8[:, b, :, 0:1].to_broadcast([P, NT, E]),
                                        ALU.subtract).then_inc(gap_ready, 1)
                for j in range(NT):
                    at = step(nc.vector.max_index(top8_at[:, b, j], top8[:, b, j], gate[:, b, j]))
                dve.wait_ge(dve_step, at)
                dve.wait_ge(pick_ready, 1)
                for j in range(NT):
                    at = step(nc.vector.tensor_tensor(
                        chosen4[:, b, j], iota_e[:].unsqueeze(2).to_broadcast([P, E, K]),
                        top8_at[:, b, j, 0:K].unsqueeze(1).to_broadcast([P, E, K]), ALU.is_equal))
                dve.wait_ge(dve_step, at)
                step(nc.vector.tensor_reduce(chosen[:, b], chosen4[:, b], AX_X, ALU.add))

            def weigh(b):
                dve.wait_ge(gexp_ready, b + 1)
                dve.wait_ge(dve_step, steps[0])
                at = step(nc.vector.tensor_tensor(gsel[:, b], gexp[:, b], chosen[:, b], ALU.mult))
                dve.wait_ge(dve_step, at)
                at = step(nc.vector.tensor_reduce(gsum[:, b], gsel[:, b], AX_X, ALU.add))
                dve.wait_ge(dve_step, at)
                at = step(nc.vector.reciprocal(grec[:, b], gsum[:, b]))
                dve.wait_ge(dve_step, at)
                at = step(nc.vector.scalar_tensor_tensor(out=route[:, b, 0], in0=gsel[:, b], scalar=ROUTE_SCALE,
                                                         in1=per_tile(grec[:, b], E), op0=ALU.mult, op1=ALU.mult))
                for k in range(2):
                    dve.wait_ge(dve_step, at)
                    at = step(nc.vector.tensor_copy(pieces[:, b, :, k], route[:, b, k]))
                    dve.wait_ge(dve_step, at)
                    at = step(nc.vector.tensor_tensor(route[:, b, k + 1], route[:, b, k], pieces[:, b, :, k], ALU.subtract))
                dve.wait_ge(dve_step, at)
                nc.vector.tensor_copy(pieces[:, b, :, 2], route[:, b, 2]).then_inc(pieces_ready, 1)

            def route_rows(b):
                dve.wait_ge(routet_ready, b + 1)
                nc.vector.tensor_copy(route_t[:, b], ps_rt[b][:].bitcast(BF16)[0:3 * E, 0:S]).then_inc(route_t_ready, 1)

            def weighted(s):
                dve.wait_ge(silu_done, s + 1)
                dve.wait_ge(rb_ready, s + 1)
                if s >= 2:
                    dve.wait_ge(z_split, s - 1)
                nc.vector.scalar_tensor_tensor(out=z[:, s % 2], in0=act_f[:, s % 3], scalar=SILU_LIMIT,
                                               in1=ps_m[s % 2][:], op0=ALU.min, op1=ALU.mult).then_inc(z_ready, 1)

            def z_low(s):
                dve.wait_ge(z_hi_ready, s + 1)
                dve.wait_ge(z_ready, s + 1)
                nc.vector.tensor_tensor(z_lo[:, s % NZ], z[:, s % 2], z_hi[:, s % NZ].bitcast(F32),
                                        ALU.subtract).then_inc(z_split, 1)

            def residual2(b):
                dve.wait_ge(yt_ready, b + 1)
                dve.wait_ge(x1_ln_ready, b + 1)
                nc.vector.tensor_tensor(y[:, b].rearrange("p j d -> p (j d)"), ps_x[:],
                                        x1_ln[:, b].rearrange("p j d -> p (j d)"), ALU.add).then_inc(y_ready, 1)

            norm1(0)
            norm1(1)
            small_operands()
            apply1(0)
            key_blocks()
            xn_low(0)
            apply1(1)
            q_low(0)
            xn_low(1)
            for j in range(NT):
                maximum(0, j)
            q_low(1)
            route_operands()
            value_blocks()
            for j in range(NT):
                maximum(1, j)
            bias_operands()
            divide(0)
            residual1(0)
            norm2(0)
            apply2(0)
            divide(1)
            t_low(0)
            choose(0)
            residual1(1)
            norm2(1)
            weigh(0)
            route_rows(0)
            apply2(1)
            weighted(0)
            weighted(1)
            for s in range(2, STEPS + 1):
                z_low(s - 2)
                if s == 3:
                    t_low(1)
                if s == 4:
                    choose(1)
                if s == 6:
                    weigh(1)
                if s == 7:
                    route_rows(1)
                if s < STEPS:
                    weighted(s)
                if s in (9, 10):
                    norm_x1(s - 9)
                if s == E + LAG + 2:
                    residual2(0)
            z_low(STEPS - 1)
            residual2(1)


def kernel(**inputs):
    import concourse.bacc as bacc
    from concourse.bass_utils import run_bass_kernel_spmd

    def array(name):
        return np.asarray(inputs[name])

    packed = np.concatenate(
        [array("ctx_1024").transpose(2, 0, 1).reshape(P, B * M)]
        + [array(f"L0_xattn_{w}").T for w in ("Wq", "Wk", "Wv", "Wo")]
        + [array("L0_ffn_gate_w").T]
        + [array(n).reshape(P, 1) for n in ("L0_xattn_bq", "L0_xattn_bk", "L0_ffn_scale")]
        + [array("L0_ffn_mlp1_b").reshape(E, P, 2)[:, :, 0].T], axis=1)
    arrays = {
        "x": array("x"),
        "packed": packed,
        "bv": array("L0_xattn_bv").reshape(1, P),
        "gate_b": array("L0_ffn_gate_b").reshape(1, E),
        "w1": array("L0_ffn_mlp1_w").reshape(E, P, 2, P).transpose(2, 3, 0, 1).reshape(2, P, E * P),
        "w2": array("L0_ffn_mlp2_w").transpose(2, 0, 1).reshape(P, E * P),
        "b2": array("L0_ffn_mlp2_b"),
    }
    nc = bacc.Bacc("TRN2", target_bir_lowering=False, num_devices=1)
    arrays = {f"{name}_dram": np.ascontiguousarray(a) for name, a in arrays.items()}
    handles = [nc.dram_tensor(name, a.shape, mybir.dt.from_np(a.dtype), kind="ExternalInput").ap()
               for name, a in arrays.items()]
    out = nc.dram_tensor("out_dram", (B, S, P), F32, kind="ExternalOutput").ap()
    build_xattn_moe(nc, *handles, out)
    result = run_bass_kernel_spmd(nc, [arrays], core_ids=[0])
    return result.results[0]["out_dram"]
```

```python
from contextlib import ExitStack

import numpy as np

import concourse.bass as bass
from concourse import mybir

F32 = mybir.dt.float32
F32R = mybir.dt.float32r
I32 = mybir.dt.int32
U32 = mybir.dt.uint32
ALU = mybir.AluOpType
ACT = mybir.ActivationFunctionType
AX_X = mybir.AxisListType.X

P = 128
B = 2
S = 512
T = B * S // P
UT = 2
UW = UT * P
U = T // UT
M = 32
H = 16
HD = P // H
NC = H * M // P
CP = 512 // UW
HC = H // NC
VW = HC * HD + HC
E = 16
K = 4
EPS = 1e-5
ALPHA = 1.702
LIMIT = 7.0
SILU_LIMIT = float(ALPHA * LIMIT / (1.0 + np.exp(-ALPHA * LIMIT)))
ROUTE_SCALE = (LIMIT + 1.0) / ALPHA
SCORE_SCALE = float(HD) ** -0.5

GROUPS = [(0, 2), (2, 2)]
STEPS = [(g, e) for g in range(len(GROUPS)) for e in range(E)]
NS = len(STEPS)
NF = 16
NW = 4
NZ = 4
NR = 6
EG = 4

DIRECT = [0, 4, 19, 20, 21, 22, 23, 24, 26, 27, 28, 29, 30]
SPLIT = [s for s in range(NS) if s not in DIRECT]

NORMS_ON_ACT = [1]

AT = [
    [0.52, 2.68, 2.69, 6.02, 10.4, 11.24, 13.99, 15.33, 16.13, 19.13,
     21.39, 24.49, 25.27, 29.51, 31.17, 33.43, 34.59, 41.02, 37.82],
    [3.8, 9.29, 9.84, 10.68, 14.73, 15.85, 18.84, 21.23, 22.77, 24.82,
     27, 30.92, 33.55, 36.03, 36.04, 38.85, 39.51, 45.49, 40.29],
    [10.23, 12.32, 14.07, 15.6, 17.05, 20.26, 24.39, 25.06, 27.89, 30.81,
     32.95, 35.38, 37.51, 38.86, 42.08, 44.09, 47.04, 58.63, 46.92],
    [22.46, 23.49, 24.87, 25.99, 28.02, 31.11, 34.26, 35.99, 36.93, 40.78,
     42.33, 45.36, 50.28, 50.29, 52.2, 54.73, 57.58, 63.92, 61.74],
]
FIRST_STEP = [1.03, 1.06]
STEP = [1.9, 2.37]
TO_WEIGH = [6.51, 3.44]
TO_LOW = [3.05, 2.84]
TO_SECOND = [3.53, 3.7]
TO_SUM = 0
TO_OUT = 4.06
EARLY = [("first_small", 0), ("keys", 0), ("key_low", 0), ("values", 0), ("keys", 1), ("value_blocks", 0),
         ("key_low", 1), ("gate_small", 0)]
EARLY_AT = [0.56, 2.79, 5.22, 8.3, 13.67, 10.52, 14.73, 13.77]
SPLIT_TIMES = [10.33, 11.72, 11.94, 17.67, 17.8, 18.59, 23.29, 26.42]
WARM = (6, 2)


SAME_BANK = [0 < g < len(GROUPS) - 1 for g in range(len(GROUPS))]


def group_end(g, at):
    units = range(GROUPS[g][0], sum(GROUPS[g]))
    return [("sum", u, at + TO_SUM) for u in units] + [("out", u, at + TO_SUM + TO_OUT) for u in units]


def program_order():
    items = [(kind, n, at) for (kind, n), at in zip(EARLY, EARLY_AT)]
    for u in range(U):
        items += [(f"stage{k}", u, at) for k, at in enumerate(AT[u][:-1])]
        items += [("route_weights", u, AT[u][-1])]
    items += [("split", n, at) for n, at in enumerate(SPLIT_TIMES)]
    first, weigh, low, second = [], [], [], []
    after = 1e-3
    for s, (g, e) in enumerate(STEPS):
        at = AT[sum(GROUPS[g]) - 1]

        def place(*earliest, times, step, buffers):
            places = list(earliest)
            if times:
                places.append(times[-1] + step)
            places += [uses[s - n] + after for uses, n in buffers if s >= n]
            return max(places)

        first.append(place(at[13] + after, times=first, step=FIRST_STEP[g], buffers=[(weigh, NF)]))
        weigh.append(place(at[17] + TO_WEIGH[g], first[s] + after, times=weigh, step=STEP[g],
                           buffers=[(second, NZ), (low, NW), (second, NW)]))
        low.append(weigh[s] + (0 if s in DIRECT else TO_LOW[g]))
        second.append(low[s] + TO_SECOND[g])
        if e == 0 and g:
            items += group_end(g - 1, second[s - 1])
            second[s] = max(second[s], second[s - 1] + (TO_SUM if SAME_BANK[g] else 0) + after)
        elif s:
            second[s] = max(second[s], second[s - 1] + after)
    items += group_end(len(GROUPS) - 1, second[-1])
    for kind, times in (("first", first), ("weigh", weigh), ("low", low), ("second", second)):
        items += [(kind, s, at) for s, at in enumerate(times) if kind != "low" or s in SPLIT]
    return [(kind, n) for kind, n, _ in sorted(items, key=lambda item: item[2])]


ORDER = program_order()

CTX0 = 0
WK0 = CTX0 + B * M
WQ0 = WK0 + P
BQ0 = WQ0 + P
BK0 = BQ0 + 1
FIRST = BK0 + 1
WV0 = 0
WO0 = WV0 + P
GW0 = WO0 + P
BV0 = GW0 + E
SC0 = BV0 + 1
GB0 = SC0 + 1
B10 = GB0 + 1
B20 = B10 + E
SECOND = B20 + P


def build_xattn_moe(nc, x, first, second, w1, w2, scratch, out):
    with ExitStack() as ctx:
        def sb(name, shape, dt=F32):
            return ctx.enter_context(nc.sbuf_tensor(name, shape, dt))

        def bank(name):
            return ctx.enter_context(nc.psum_tensor(name, [P, 512], F32))

        def sem(name):
            return ctx.enter_context(nc.semaphore(name))

        ps_x = bank("ps_x")
        ps_q = bank("ps_q")
        ps_r = [bank("ps_r0"), bank("ps_r1")]
        ps_t, ps_g = ps_r
        ps_y = [ps_x, ps_t]
        ps_o = bank("ps_o")
        ps_h = [bank("ps_h0"), bank("ps_h1")]
        ps_a = bank("ps_a")
        ps_acc = [ps_a] * (len(GROUPS) - 1) + [ps_o]

        x_sb = sb("x_sb", [P, T, P])
        pk1 = sb("pk1", [P, FIRST])
        pk2 = sb("pk2", [P, SECOND])
        w1_sb = sb("w1_sb", [P, E * P])
        w2_sb = sb("w2_sb", [P, E * P])
        w1_hi = sb("w1_hi", [P, E * P], F32R)
        w1_lo = sb("w1_lo", [P, E * P], F32R)
        w2_hi = sb("w2_hi", [P, E * P], F32R)
        w2_lo = sb("w2_lo", [P, E * P], F32R)

        ident = sb("ident", [P, P])
        key_mask = sb("key_mask", [P, H])
        val_mask = sb("val_mask", [P, HC])
        neg_expand = sb("neg_expand", [H, H * M], F32R)
        pair_eye = sb("pair_eye", [2 * E, E])
        iota_e = sb("iota_e", [P, E], I32)
        neg_half = sb("neg_half", [P, UT])
        euler = sb("euler", [P, UT, K - 1])

        gw = sb("gw", [P, 2 * E], F32R)
        b1_scaled = sb("b1_scaled", [P, E])
        b2_scaled = sb("b2_scaled", [E, P])
        ctx_rep = sb("ctx_rep", [P, B, HC, M])
        kbd = sb("kbd", [P, B, H * M])
        kbd_hi = sb("kbd_hi", [P, B, H * M], F32R)
        kbd_lo = sb("kbd_lo", [P, B, H * M], F32R)
        vbd = sb("vbd", [P, B, NC, VW])

        stats = sb("stats", [P, 2 * U, UT, 6])
        moments = sb("moments", [P, 2 * U, UT, 2])
        spread = sb("spread", [P, 3 * U, UT])
        rstd = sb("rstd", [P, 3 * U, UT])
        neg_mean = sb("neg_mean", [P, 2 * U, UT])
        shift = sb("shift", [P, 2 * U, UT])
        ln_scale = sb("ln_scale", [P, U, UT])
        ln_shift = sb("ln_shift", [P, U, UT])
        ln_prod = sb("ln_prod", [P, U, UT])

        xn = sb("xn", [P, T, P])
        xn_t = sb("xn_t", [P, 2, UW])
        q_hi = sb("q_hi", [P, 2, UW], F32R)
        q_lo = sb("q_lo", [P, 2, UW], F32R)
        row_max = sb("row_max", [P, T, H])
        max_t = sb("max_t", [H, U, UW], F32R)
        probs = sb("probs", [P, 2, NC, UW])
        rden = sb("rden", [P, U, UT * H])
        attn = sb("attn", [P, T, P])
        attn_t = sb("attn_t", [P, U, UW])
        x1 = sb("x1", [P, T, P])
        x1_ln = sb("x1_ln", [P, T, P])
        t_hi = sb("t_hi", [P, U * UW], F32R)
        t_lo = sb("t_lo", [P, U * UW], F32R)

        gate_t = sb("gate_t", [2 * E, U, UW])
        top8 = sb("top8", [P, T, 8])
        top8_at = sb("top8_at", [P, T, 8], U32)
        chosen = sb("chosen", [P, T, E, K])
        gap = sb("gap", [P, T, K - 1])
        gexp = sb("gexp", [P, T, K])
        gexp_at = sb("gexp_at", [P, T, E, K])
        gsel = sb("gsel", [P, T, E])
        gsum = sb("gsum", [P, T])
        grec = sb("grec", [P, T])
        route = sb("route", [P, T, E])
        route_t = sb("route_t", [E, U * UW])
        row_all = sb("row_all", [P, NR, 512])

        act_f = sb("act_f", [P, NF, 512])
        z = sb("z", [P, NW, 512])
        z_hi = sb("z_hi", [P, NZ, 512], F32R)
        z_lo = sb("z_lo", [P, NZ, 512], F32R)
        acc_t = sb("acc_t", [P, U * UW])

        x_in = [sem(f"x_in{u}") for u in range(U)]
        first_in = sem("first_in")
        second_in = sem("second_in")
        w1_in = [sem(f"w1_in{h}") for h in range(2)]
        w2_in = [sem(f"w2_in{h}") for h in range(2)]
        rows_out = [sem(f"rows_out{u}") for u in range(U)]
        row_in = [sem(f"row_in{n}") for n in range(NR)]
        out_done = sem("out_done")
        pool_step = sem("pool_step")
        dve_step = sem("dve_step")
        ident_ready = sem("ident_ready")
        masks_ready = sem("masks_ready")
        consts_ready = sem("consts_ready")
        rstd_ready = sem("rstd_ready")
        weights_hi = sem("weights_hi")
        weights_split = sem("weights_split")
        ctx_rep_ready = sem("ctx_rep_ready")
        gw_split = sem("gw_split")
        biases_ready = sem("biases_ready")
        k_ready = sem("k_ready")
        v_ready = sem("v_ready")
        kbd_made = sem("kbd_made")
        kbd_hi_ready = sem("kbd_hi_ready")
        kbd_split = sem("kbd_split")
        vbd_ready = sem("vbd_ready")
        spread_ready = sem("spread_ready")
        xn_ready = [sem(f"xn_ready{u}") for u in range(U)]
        xnt_ready = sem("xnt_ready")
        xn_t_ready = sem("xn_t_ready")
        q_ready = sem("q_ready")
        q_hi_ready = sem("q_hi_ready")
        q_split = sem("q_split")
        mscore_ready = sem("mscore_ready")
        max_done = sem("max_done")
        maxt_ready = sem("maxt_ready")
        max_t_ready = sem("max_t_ready")
        score_ready = sem("score_ready")
        exp_done = sem("exp_done")
        o_ready = sem("o_ready")
        attn_ready = sem("attn_ready")
        attnt_ready = sem("attnt_ready")
        attn_t_ready = sem("attn_t_ready")
        proj_ready = sem("proj_ready")
        x1_ready = sem("x1_ready")
        xc_ready = [sem(f"xc_ready{u}") for u in range(U)]
        x1_ln_ready = sem("x1_ln_ready")
        tt_ready = sem("tt_ready")
        t_hi_ready = sem("t_hi_ready")
        t_split = sem("t_split")
        gatet_ready = sem("gatet_ready")
        gate_t_ready = sem("gate_t_ready")
        gate_ready = sem("gate_ready")
        gate_read = sem("gate_read")
        gap_ready = sem("gap_ready")
        gexp_ready = sem("gexp_ready")
        route_ready = sem("route_ready")
        routet_ready = sem("routet_ready")
        route_t_ready = sem("route_t_ready")
        h_ready = sem("h_ready")
        silu_done = sem("silu_done")
        z_ready = sem("z_ready")
        z_hi_ready = sem("z_hi_ready")
        z_split = sem("z_split")
        mlp2_done = sem("mlp2_done")
        acc_t_ready = [sem(f"acc_t_ready{u}") for u in range(U)]
        yt_ready = sem("yt_ready")
        y_ready = sem("y_ready")

        x_tiles = x.rearrange("b (j p) d -> p (b j) d", p=P)
        out_tiles = out.rearrange("b (j p) d -> p (b j) d", p=P)
        half = E * P // 2

        def tiles(u):
            return range(u * UT, (u + 1) * UT)

        def group(g):
            u, n = GROUPS[g]
            return slice(u * UW, (u + n) * UW), n * UW, slice(u * UT, (u + n) * UT)

        unit_group = [g for g, (_, n) in enumerate(GROUPS) for _ in range(n)]

        def unit_sum(u):
            g = unit_group[u]
            at = (u - GROUPS[g][0]) * UW
            return ps_acc[g][:, at:at + UW], slice(u * UW, (u + 1) * UW)

        def norm_operands(n):
            u = n % U
            src, ready = (x_sb, xn_ready[u]) if n < U else (x1, xc_ready[u])
            return [(xn[:, t], src[:, t]) for t in tiles(u)], ready

        norms = [n if kind == "stage0" else U + n for kind, n in ORDER if kind in ("stage0", "stage11")]

        def last_unit(g):
            return GROUPS[g][0] + GROUPS[g][1] - 1

        block = ctx.enter_context(nc.Block())

        @block.sync
        def _(sp):
            for u in range(U):
                sp.dma_start(x_sb[:, u * UT:(u + 1) * UT], x_tiles[:, u * UT:(u + 1) * UT]).then_inc(x_in[u], 16)
                if u == 0:
                    sp.dma_start(pk2[:], second).then_inc(second_in, 16)
            for h in range(2):
                cols = slice(h * half, (h + 1) * half)
                sp.dma_start(w1_sb[:, cols], w1[0, :, cols]).then_inc(w1_in[h], 16)
                sp.dma_start(w2_sb[:, cols], w2[:, cols]).then_inc(w2_in[h], 16)

            def store(g):
                for u in range(GROUPS[g][0], last_unit(g) + 1):
                    ts = slice(u * UT, (u + 1) * UT)
                    sp.wait_ge(y_ready, u + 1)
                    sp.dma_start(out_tiles[:, ts], x_sb[:, ts]).then_inc(out_done, 16)

            s = 0
            for g in range(len(GROUPS)):
                for u in range(GROUPS[g][0], last_unit(g) + 1):
                    sp.wait_ge(route_t_ready, u + 1)
                    cols = slice(u * UW, (u + 1) * UW)
                    sp.dma_start(scratch[:, cols], route_t[:, cols]).then_inc(rows_out[u], 16)
                for u in range(GROUPS[g][0], last_unit(g) + 1):
                    sp.wait_ge(rows_out[u], 16)
                cols, width, _ = group(g)
                for e in range(E):
                    if s >= NR:
                        sp.wait_ge(z_ready, s - NR + 1)
                    sp.dma_start(row_all[:, s % NR, 0:width],
                                 scratch[e:e + 1, cols].to_broadcast([P, width])).then_inc(row_in[s % NR], 16)
                    s += 1
                    if g and e == E // 2:
                        store(g - 1)
            store(len(GROUPS) - 1)
            sp.wait_ge(out_done, 16 * U)

        @block.gpsimd
        def _(pool):
            nc.gpsimd.memset(neg_half[:], -0.5).then_inc(pool_step, 1)
            nc.gpsimd.memset(euler[:], float(np.e)).then_inc(pool_step, 1)
            nc.gpsimd.memset(gexp[:], 1.0).then_inc(pool_step, 1)
            nc.gpsimd.memset(ident[:], 0.0).then_inc(pool_step, 1)
            nc.gpsimd.memset(key_mask[:], 1.0).then_inc(pool_step, 1)
            nc.gpsimd.memset(val_mask[:], 1.0).then_inc(pool_step, 1)
            nc.gpsimd.memset(pair_eye[:], 0.0).then_inc(pool_step, 1)
            done = 7
            pool.wait_ge(pool_step, done)
            nc.gpsimd.affine_select(out=ident[:], in_=ident[:], compare_op=ALU.not_equal, fill=1.0,
                                    base=0, pattern=[[-1, P]], channel_multiplier=1).then_inc(ident_ready, 1)
            nc.gpsimd.affine_select(out=key_mask[:], in_=key_mask[:], compare_op=ALU.is_ge, fill=0.0,
                                    base=0, pattern=[[-HD, H]], channel_multiplier=1).then_inc(pool_step, 1)
            nc.gpsimd.affine_select(out=val_mask[:], in_=val_mask[:], compare_op=ALU.is_ge, fill=0.0,
                                    base=0, pattern=[[-M, HC]], channel_multiplier=1).then_inc(pool_step, 1)
            done += 2
            pool.wait_ge(pool_step, done)
            nc.gpsimd.affine_select(out=key_mask[:], in_=key_mask[:], compare_op=ALU.is_ge, fill=0.0,
                                    base=HD - 1, pattern=[[HD, H]], channel_multiplier=-1).then_inc(masks_ready, 1)
            nc.gpsimd.affine_select(out=val_mask[:], in_=val_mask[:], compare_op=ALU.is_ge, fill=0.0,
                                    base=M - 1, pattern=[[M, HC]], channel_multiplier=-1).then_inc(masks_ready, 1)

            def power_step(instruction):
                nonlocal done
                done += 1
                instruction.then_inc(pool_step, 1)
                return done

            def inverse_root(n, count):
                pool.wait_ge(spread_ready, count)
                if n in NORMS_ON_ACT:
                    power_step(nc.gpsimd.tensor_tensor(rstd[:, n], spread[:, n], neg_half[:], ALU.pow))
                    at = power_step(nc.gpsimd.tensor_scalar(neg_mean[:, n], moments[:, n, :, 0], -1.0, None, ALU.mult))
                    pool.wait_ge(pool_step, at)
                    nc.gpsimd.tensor_tensor(shift[:, n], neg_mean[:, n], rstd[:, n], ALU.mult).then_inc(rstd_ready, 1)
                else:
                    nc.gpsimd.tensor_tensor(rstd[:, n], spread[:, n], neg_half[:], ALU.pow).then_inc(rstd_ready, 1)

            def residual_terms(u):
                power_step(nc.gpsimd.tensor_tensor(rstd[:, 2 * U + u], spread[:, 2 * U + u], neg_half[:], ALU.pow))
                pool.wait_ge(pool_step, done)
                power_step(nc.gpsimd.tensor_scalar(ln_scale[:, u], rstd[:, 2 * U + u], 1.0, None, ALU.add))
                power_step(nc.gpsimd.tensor_tensor(ln_prod[:, u], moments[:, U + u, :, 0], rstd[:, 2 * U + u], ALU.mult))
                pool.wait_ge(pool_step, done)
                power_step(nc.gpsimd.tensor_scalar(ln_shift[:, u], ln_prod[:, u], -1.0, None, ALU.mult))
                pool.wait_ge(pool_step, done)
                for j, t in enumerate(tiles(u)):
                    last = nc.gpsimd.tensor_scalar(x1_ln[:, t], x1[:, t], ln_scale[:, u, j:j + 1],
                                                   ln_shift[:, u, j:j + 1], ALU.mult, ALU.add)
                last.then_inc(x1_ln_ready, 1)

            def expand_constants():
                power_step(nc.gpsimd.memset(neg_expand[:].bitcast(F32), -1.0))
                pool.wait_ge(pool_step, done)
                nc.gpsimd.affine_select(out=neg_expand[:], in_=neg_expand[:].bitcast(F32), compare_op=ALU.is_equal,
                                        fill=0.0, base=0, pattern=[[-1, H], [0, M]],
                                        channel_multiplier=1).then_inc(consts_ready, 1)
                for k in range(2):
                    at = power_step(nc.gpsimd.affine_select(
                        out=pair_eye[:], in_=pair_eye[:], compare_op=ALU.not_equal, fill=1.0,
                        base=-E * k, pattern=[[-1, E]], channel_multiplier=1))
                    pool.wait_ge(pool_step, at)
                nc.gpsimd.iota(iota_e[:], pattern=[[1, E]], base=0, channel_multiplier=0).then_inc(consts_ready, 1)

            def kbd_low(b):
                pool.wait_ge(kbd_hi_ready, b + 1)
                nc.gpsimd.tensor_tensor(kbd_lo[:, b], kbd[:, b], kbd_hi[:, b].bitcast(F32), ALU.subtract).then_inc(kbd_split, 1)

            def weights_low(n):
                w, hi, lo = ((w1_sb, w1_hi, w1_lo), (w2_sb, w2_hi, w2_lo))[n % 2]
                cols = slice(n // 2 * EG * P, (n // 2 + 1) * EG * P)
                pool.wait_ge(weights_hi, n + 1)
                nc.gpsimd.tensor_tensor(lo[:, cols], w[:, cols], hi[:, cols].bitcast(F32),
                                        ALU.subtract).then_inc(weights_split, 1)

            for kind, n in ORDER:
                if kind == "stage0":
                    inverse_root(n, norms.index(n) + 1)
                if kind == "stage11":
                    inverse_root(U + n, norms.index(U + n) + 1)
                if kind == "stage15":
                    ts = slice(n * UT, (n + 1) * UT)
                    pool.wait_ge(gap_ready, n + 1)
                    nc.gpsimd.tensor_tensor(gexp[:, ts, 1:K], euler[:], gap[:, ts], ALU.pow).then_inc(gexp_ready, 1)
                if kind == "stage16":
                    residual_terms(n)
                if kind == "first_small":
                    expand_constants()
                if kind == "key_low":
                    kbd_low(n)
                if kind == "split":
                    weights_low(n)

        @block.tensor
        def _(pe):
            mm, tr = nc.tensor.matmul, nc.tensor.transpose

            def split_product(acc, lhs_hi, lhs_lo, rhs_hi, rhs_lo, start=True, stop=True):
                mm(acc, lhs_hi, rhs_hi, start=start, stop=False)
                mm(acc, lhs_hi, rhs_lo, start=False, stop=False)
                return mm(acc, lhs_lo, rhs_hi, start=False, stop=stop)

            def project_keys():
                pe.wait_ge(first_in, 16)
                mm(ps_o[:, 0:B * M], pk1[:, WK0:WK0 + P], pk1[:, CTX0:CTX0 + B * M],
                   start=True, stop=True).then_inc(k_ready, 1)

            def project_values():
                pe.wait_ge(second_in, 16)
                pe.wait_ge(ctx_rep_ready, 1)
                for b in range(B):
                    last = mm(ps_a[:, b * P:(b + 1) * P], ctx_rep[:, b].rearrange("p a m -> p (a m)"),
                              pk2[:, WV0:WV0 + P], start=True, stop=True)
                last.then_inc(v_ready, 1)

            readers = {}

            def claim(bank, reader, value):
                if bank.name in readers:
                    pe.wait_ge(*readers[bank.name])
                readers[bank.name] = (reader, value)

            def transposes(bank, src, ready, value, rows, signal):
                pe.wait_ge(ready, value)
                for j, tile in enumerate(src):
                    last = tr(bank[0:rows, j * P:(j + 1) * P], tile, ident[:])
                last.then_inc(signal, 1)

            def attention_stage(u, stage):
                b = u * UW // S
                if stage == 2:
                    claim(ps_x, xn_t_ready, u + 1)
                    transposes(ps_x, [xn[:, t] for t in tiles(u)], xn_ready[u], 1, P, xnt_ready)
                if stage == 3:
                    claim(ps_q, q_split, u + 1)
                    pe.wait_ge(xn_t_ready, u + 1)
                    mm(ps_q[:, 0:UW], pk1[:, WQ0:WQ0 + P], xn_t[:, u % 2], start=True, stop=True).then_inc(q_ready, 1)
                if stage == 4:
                    pe.wait_ge(q_split, u + 1)
                    pe.wait_ge(kbd_hi_ready, b + 1)
                    for j, t in enumerate(tiles(u)):
                        if t >= 2:
                            pe.wait_ge(max_done, t - 1)
                        mm(ps_h[t % 2][:], q_hi[:, u % 2, j * P:(j + 1) * P], kbd_hi[:, b],
                           start=True, stop=True).then_inc(mscore_ready, 1)
                if stage == 5:
                    claim(ps_x, max_t_ready, u + 1)
                    transposes(ps_x, [row_max[:, t] for t in tiles(u)], max_done, UT * (u + 1), H, maxt_ready)
                if stage in (6, 7):
                    i = stage - 6
                    pe.wait_ge(kbd_split, b + 1)
                    pe.wait_ge(consts_ready, 1)
                    n = 2 * u + i
                    claim(ps_r[n % 2], exp_done, n + 1)
                    for k in range(CP):
                        cols = slice((i * CP + k) * P, (i * CP + k + 1) * P)
                        acc = ps_r[n % 2][:, k * UW:(k + 1) * UW]
                        split_product(acc, kbd_hi[:, b, cols], kbd_lo[:, b, cols], q_hi[:, u % 2], q_lo[:, u % 2], stop=False)
                        if i == 0 and k == 0:
                            pe.wait_ge(max_t_ready, u + 1)
                        last = mm(acc, neg_expand[:, cols], max_t[:, u], start=False, stop=True)
                    last.then_inc(score_ready, 1)
                if stage in (8, 9):
                    i = stage - 8
                    pe.wait_ge(exp_done, 2 * u + i + 1)
                    pe.wait_ge(vbd_ready, B)
                    if i == 0 and u:
                        pe.wait_ge(attn_ready, u)
                    for c in range(i * CP, (i + 1) * CP):
                        for j in range(UT):
                            at = (j * NC + c) * VW
                            last = mm(ps_o[:, at:at + VW], probs[:, u % 2, c, j * P:(j + 1) * P], vbd[:, b, c],
                                      start=True, stop=True)
                    last.then_inc(o_ready, 1)
                if stage == 10:
                    claim(ps_x, attn_t_ready, u + 1)
                    transposes(ps_x, [attn[:, t] for t in tiles(u)], attn_ready, u + 1, P, attnt_ready)
                if stage == 11:
                    claim(ps_q, x1_ready, u + 1)
                    pe.wait_ge(attn_t_ready, u + 1)
                    for j in range(UT):
                        last = mm(ps_q[:, j * P:(j + 1) * P], attn_t[:, u, j * P:(j + 1) * P], pk2[:, WO0:WO0 + P],
                                  start=True, stop=True)
                    last.then_inc(proj_ready, 1)
                if stage == 13:
                    claim(ps_t, t_split, u + 1)
                    transposes(ps_t, [xn[:, t] for t in tiles(u)], xc_ready[u], 1, P, tt_ready)
                if stage == 14:
                    claim(ps_g, gate_t_ready, u + 1)
                    pe.wait_ge(t_split, u + 1)
                    pe.wait_ge(gw_split, 1)
                    cols = slice(u * UW, (u + 1) * UW)
                    mm(ps_g[0:2 * E, 0:UW], gw[:], t_hi[:, cols], start=True, stop=False)
                    mm(ps_g[0:2 * E, 0:UW], gw[:], t_lo[:, cols], start=False, stop=True).then_inc(gatet_ready, 1)
                if stage == 15:
                    claim(ps_g, gate_read, u + 1)
                    pe.wait_ge(gate_t_ready, u + 1)
                    pe.wait_ge(consts_ready, 2)
                    for j in range(UT):
                        last = mm(ps_g[:, j * E:(j + 1) * E], gate_t[:, u, j * P:(j + 1) * P], pair_eye[:],
                                  start=True, stop=True)
                    last.then_inc(gate_ready, 1)
                if stage == 17:
                    claim(ps_g, route_t_ready, u + 1)
                    pe.wait_ge(route_ready, u + 1)
                    for j, t in enumerate(tiles(u)):
                        last = tr(ps_g[0:E, j * P:(j + 1) * P], route[:, t], ident[:])
                    last.then_inc(routet_ready, 1)

            def mlp1(s):
                g, e = STEPS[s]
                cols, width, _ = group(g)
                ecols = slice(e * P, (e + 1) * P)
                if e == 0:
                    pe.wait_ge(t_split, last_unit(g) + 1)
                if g == 0 and e % EG == 0:
                    pe.wait_ge(weights_split, 2 * (e // EG) + 1)
                if s >= 2:
                    pe.wait_ge(silu_done, s - 1)
                else:
                    pe.wait_ge(max_done, T)
                split_product(ps_h[s % 2][:, 0:width], w1_hi[:, ecols], w1_lo[:, ecols],
                              t_hi[:, cols], t_lo[:, cols]).then_inc(h_ready, 1)

            def mlp2(s):
                g, e = STEPS[s]
                cols, width, _ = group(g)
                ecols = slice(e * P, (e + 1) * P)
                acc = ps_acc[g][:, 0:width]
                if e == 0:
                    pe.wait_ge(biases_ready, 2)
                    pe.wait_ge(route_t_ready, last_unit(g) + 1)
                    if SAME_BANK[g]:
                        for u in range(GROUPS[g - 1][0], last_unit(g - 1) + 1):
                            pe.wait_ge(acc_t_ready[u], 1)
                    if ps_acc[g] is ps_o:
                        pe.wait_ge(attn_ready, U)
                    mm(acc, b2_scaled[:], route_t[:, cols], start=True, stop=False)
                if s in DIRECT:
                    if g == 0:
                        pe.wait_ge(w2_in[e * P // half], 16)
                    pe.wait_ge(z_ready, s + 1)
                    last = mm(acc, w2_sb[:, ecols], z[:, s % NW, 0:width], start=False, stop=(e == E - 1))
                else:
                    n = SPLIT.index(s)
                    pe.wait_ge(weights_split, 2 * (e // EG) + 2)
                    pe.wait_ge(z_split, n + 1)
                    last = split_product(acc, w2_hi[:, ecols], w2_lo[:, ecols], z_hi[:, n % NZ, 0:width],
                                         z_lo[:, n % NZ, 0:width], start=False, stop=(e == E - 1))
                last.then_inc(mlp2_done, 1)

            def transpose_y(u):
                claim(ps_y[u % 2], y_ready, u + 1)
                transposes(ps_y[u % 2], [acc_t[:, t * P:(t + 1) * P] for t in tiles(u)], acc_t_ready[u], 1, P, yt_ready)

            def warm_up(n):
                for _ in range(n):
                    mm(ps_h[0][:, 0:P], ident[:], ident[:], start=True, stop=True)

            pe.wait_ge(ident_ready, 1)
            warm_up(WARM[0])
            project_keys()
            warm_up(WARM[1])
            for kind, n in ORDER:
                if kind.startswith("stage"):
                    attention_stage(n, int(kind[5:]))
                if kind == "values":
                    project_values()
                if kind == "first":
                    mlp1(n)
                if kind == "second":
                    mlp2(n)
                if kind == "out":
                    transpose_y(n)

        @block.scalar
        def _(act):
            act.dma_start(pk1[:], first).then_inc(first_in, 16)

            def weights_high(n):
                w, hi, arrived = ((w1_sb, w1_hi, w1_in), (w2_sb, w2_hi, w2_in))[n % 2]
                cols = slice(n // 2 * EG * P, (n // 2 + 1) * EG * P)
                act.wait_ge(arrived[n // 2 * EG * P // half], 16)
                nc.scalar.activation(hi[:, cols], w[:, cols], ACT.Copy).then_inc(weights_hi, 1)

            def kbd_high(b):
                act.wait_ge(kbd_made, b + 1)
                nc.scalar.activation(kbd_hi[:, b], kbd[:, b], ACT.Copy).then_inc(kbd_hi_ready, 1)

            def apply_norm(n):
                if n not in NORMS_ON_ACT:
                    return
                if n < U:
                    act.wait_ge(x_in[n], 16)
                act.wait_ge(rstd_ready, norms.index(n) + 1)
                pairs, ready = norm_operands(n)
                for j, (dst, src) in enumerate(pairs):
                    last = nc.scalar.activation(dst, src, ACT.Identity, scale=rstd[:, n, j:j + 1],
                                                bias=shift[:, n, j:j + 1])
                last.then_inc(ready, 1)

            def attention_stage(u, stage):
                if stage == 1:
                    apply_norm(u)
                if stage == 2:
                    act.wait_ge(xnt_ready, u + 1)
                    nc.scalar.activation(xn_t[:, u % 2], ps_x[:, 0:UW], ACT.Copy).then_inc(xn_t_ready, 1)
                if stage == 3:
                    act.wait_ge(q_ready, u + 1)
                    nc.scalar.activation(q_hi[:, u % 2], ps_q[:, 0:UW], ACT.Identity,
                                         bias=pk1[:, BQ0:BQ0 + 1]).then_inc(q_hi_ready, 1)
                if stage == 5:
                    act.wait_ge(maxt_ready, u + 1)
                    nc.scalar.activation(max_t[:, u], ps_x[0:H, 0:UW], ACT.Copy).then_inc(max_t_ready, 1)
                if stage in (6, 7):
                    i = stage - 6
                    n = 2 * u + i
                    act.wait_ge(score_ready, n + 1)
                    if u >= 2 and i == 0:
                        act.wait_ge(o_ready, 2 * (u - 1))
                    nc.scalar.activation(probs[:, u % 2, i * CP:(i + 1) * CP].rearrange("p c n -> p (c n)"),
                                         ps_r[n % 2][:], ACT.Exp, scale=SCORE_SCALE).then_inc(exp_done, 1)
                if stage == 10:
                    act.wait_ge(attnt_ready, u + 1)
                    nc.scalar.activation(attn_t[:, u], ps_x[:, 0:UW], ACT.Identity,
                                         bias=pk2[:, BV0:BV0 + 1]).then_inc(attn_t_ready, 1)
                if stage == 12:
                    apply_norm(U + u)
                if stage == 13:
                    act.wait_ge(tt_ready, u + 1)
                    nc.scalar.activation(t_hi[:, u * UW:(u + 1) * UW], ps_t[:, 0:UW], ACT.Copy,
                                         scale=pk2[:, SC0:SC0 + 1]).then_inc(t_hi_ready, 1)
                if stage == 14:
                    act.wait_ge(gatet_ready, u + 1)
                    nc.scalar.activation(gate_t[:, u], ps_g[0:2 * E, 0:UW], ACT.Identity,
                                         bias=pk2[0:2 * E, GB0:GB0 + 1]).then_inc(gate_t_ready, 1)
                if stage == 17:
                    act.wait_ge(routet_ready, u + 1)
                    nc.scalar.activation(route_t[:, u * UW:(u + 1) * UW], ps_g[0:E, 0:UW],
                                         ACT.Copy).then_inc(route_t_ready, 1)

            def silu(s):
                g, e = STEPS[s]
                width = group(g)[1]
                act.wait_ge(h_ready, s + 1)
                if s == 0:
                    act.wait_ge(biases_ready, 1)
                if s >= NF:
                    act.wait_ge(z_ready, s - NF + 1)
                nc.scalar.activation(act_f[:, s % NF, 0:width], ps_h[s % 2][:, 0:width], ACT.Silu, scale=ALPHA,
                                     bias=b1_scaled[:, e:e + 1]).then_inc(silu_done, 1)

            def z_high(s):
                width = group(STEPS[s][0])[1]
                n = SPLIT.index(s)
                act.wait_ge(z_ready, s + 1)
                if n >= NZ:
                    act.wait_ge(mlp2_done, SPLIT[n - NZ] + 1)
                nc.scalar.activation(z_hi[:, n % NZ, 0:width], z[:, s % NW, 0:width], ACT.Copy).then_inc(z_hi_ready, 1)

            def acc_copy(u):
                act.wait_ge(mlp2_done, E * (unit_group[u] + 1))
                acc, cols = unit_sum(u)
                nc.scalar.activation(acc_t[:, cols], acc, ACT.Copy).then_inc(acc_t_ready[u], 1)

            for kind, n in ORDER:
                if kind.startswith("stage"):
                    attention_stage(n, int(kind[5:]))
                if kind == "key_low":
                    kbd_high(n)
                if kind == "split":
                    weights_high(n)
                if kind == "first":
                    silu(n)
                if kind == "weigh" and n in SPLIT:
                    z_high(n)
                if kind == "sum":
                    acc_copy(n)

        @block.vector
        def _(dve):
            count = [0]

            def step(instruction):
                count[0] += 1
                instruction.then_inc(dve_step, 1)
                return count[0]

            def normalise(n, src, scale, shift):
                for j in range(UT):
                    at = step(nc.vector.bn_stats(stats[:, n, j], src(j)))
                dve.wait_ge(dve_step, at)
                for j in range(UT):
                    at = step(nc.vector.bn_aggr(moments[:, n, j], stats[:, n, j]))
                dve.wait_ge(dve_step, at)
                if n >= U:
                    nc.vector.tensor_scalar(spread[:, U + n], moments[:, n, :, 1], EPS, None, ALU.add).then_inc(dve_step, 1)
                    count[0] += 1
                nc.vector.tensor_scalar(spread[:, n], moments[:, n, :, 1], scale, shift,
                                        ALU.mult, ALU.add).then_inc(spread_ready, 1)

            def apply_norm(n):
                if n in NORMS_ON_ACT:
                    return
                dve.wait_ge(rstd_ready, norms.index(n) + 1)
                pairs, ready = norm_operands(n)
                for j, (dst, src) in enumerate(pairs):
                    last = nc.vector.tensor_scalar(dst, src, moments[:, n, j, 0:1], rstd[:, n, j:j + 1],
                                                   ALU.subtract, ALU.mult)
                last.then_inc(ready, 1)

            def small_operands():
                dve.wait_ge(first_in, 16)
                nc.vector.tensor_copy(ctx_rep[:], pk1[:, CTX0:CTX0 + B * M].rearrange("p (b m) -> p b m", b=B)
                                      .unsqueeze(2).to_broadcast([P, B, HC, M])).then_inc(ctx_rep_ready, 1)

            def key_block(b):
                dve.wait_ge(k_ready, 1)
                dve.wait_ge(masks_ready, 2)
                nc.vector.scalar_tensor_tensor(
                    out=kbd[:, b].rearrange("p (h m) -> p h m", h=H),
                    in0=ps_o[:, b * M:(b + 1) * M].unsqueeze(1).to_broadcast([P, H, M]),
                    scalar=pk1[:, BK0:BK0 + 1], in1=key_mask[:].unsqueeze(2).to_broadcast([P, H, M]),
                    op0=ALU.add, op1=ALU.mult).then_inc(kbd_made, 1)

            def value_blocks():
                dve.wait_ge(v_ready, 1)
                for b in range(B):
                    step(nc.vector.tensor_tensor(
                        vbd[:, b, :, 0:HC * HD].rearrange("p c (a d) -> p c a d", a=HC),
                        ps_a[:, b * P:(b + 1) * P].rearrange("p (c a d) -> p c a d", c=NC, a=HC),
                        val_mask[:].unsqueeze(1).unsqueeze(3).to_broadcast([P, NC, HC, HD]), ALU.mult))
                    nc.vector.tensor_copy(vbd[:, b, :, HC * HD:VW],
                                          val_mask[:].unsqueeze(1).to_broadcast([P, NC, HC])).then_inc(vbd_ready, 1)

            def gate_and_biases():
                dve.wait_ge(second_in, 16)
                at = step(nc.vector.tensor_copy(gw[:, 0:E], pk2[:, GW0:GW0 + E]))
                nc.vector.tensor_scalar(b1_scaled[:], pk2[:, B10:B10 + E], ALPHA, None, ALU.mult).then_inc(biases_ready, 1)
                nc.vector.tensor_scalar(b2_scaled[:], pk2[0:E, B20:B20 + P], 1.0 / ROUTE_SCALE, None,
                                        ALU.mult).then_inc(biases_ready, 1)
                dve.wait_ge(dve_step, at)
                nc.vector.tensor_tensor(gw[:, E:2 * E], pk2[:, GW0:GW0 + E], gw[:, 0:E].bitcast(F32),
                                        ALU.subtract).then_inc(gw_split, 1)

            chosen_at = {}

            def choose(u):
                ts = slice(u * UT, (u + 1) * UT)
                logits = ps_g[:, 0:UT * E].rearrange("p (j e) -> p j e", e=E)
                dve.wait_ge(gate_ready, u + 1)
                for j, t in enumerate(tiles(u)):
                    at = step(nc.vector.max(top8[:, t], logits[:, j]))
                dve.wait_ge(dve_step, at)
                nc.vector.tensor_tensor(gap[:, ts], top8[:, ts, 1:K], top8[:, ts, 0:1].to_broadcast([P, UT, K - 1]),
                                        ALU.subtract).then_inc(gap_ready, 1)
                for j, t in enumerate(tiles(u)):
                    last = nc.vector.max_index(top8_at[:, t], top8[:, t], logits[:, j])
                last.then_inc(gate_read, 1)
                dve.wait_ge(gate_read, u + 1)
                dve.wait_ge(consts_ready, 2)
                for t in tiles(u):
                    chosen_at[u] = step(nc.vector.tensor_tensor(
                        chosen[:, t], iota_e[:].unsqueeze(2).to_broadcast([P, E, K]),
                        top8_at[:, t, 0:K].unsqueeze(1).to_broadcast([P, E, K]), ALU.is_equal))

            def route_weights(u):
                ts = slice(u * UT, (u + 1) * UT)
                dve.wait_ge(gexp_ready, u + 1)
                dve.wait_ge(dve_step, chosen_at[u])
                sum_at = step(nc.vector.tensor_reduce(gsum[:, ts], gexp[:, ts], AX_X, ALU.add))
                at = step(nc.vector.tensor_tensor(gexp_at[:, ts], chosen[:, ts],
                                                  gexp[:, ts].unsqueeze(2).to_broadcast([P, UT, E, K]), ALU.mult))
                dve.wait_ge(dve_step, sum_at)
                step(nc.vector.reciprocal(grec[:, ts], gsum[:, ts]))
                dve.wait_ge(dve_step, at)
                at = step(nc.vector.tensor_reduce(gsel[:, ts], gexp_at[:, ts], AX_X, ALU.add))
                dve.wait_ge(dve_step, at)
                nc.vector.scalar_tensor_tensor(out=route[:, ts], in0=gsel[:, ts], scalar=ROUTE_SCALE,
                                               in1=grec[:, ts].unsqueeze(2).to_broadcast([P, UT, E]),
                                               op0=ALU.mult, op1=ALU.mult).then_inc(route_ready, 1)

            def attention_stage(u, stage):
                ts = slice(u * UT, (u + 1) * UT)
                cols = slice(u * UW, (u + 1) * UW)
                if stage == 0:
                    dve.wait_ge(x_in[u], 16)
                    normalise(u, lambda j: x_sb[:, u * UT + j], 1.0, EPS)
                if stage == 1:
                    apply_norm(u)
                if stage == 3:
                    dve.wait_ge(q_hi_ready, u + 1)
                    nc.vector.scalar_tensor_tensor(out=q_lo[:, u % 2], in0=ps_q[:, 0:UW], scalar=pk1[:, BQ0:BQ0 + 1],
                                                   in1=q_hi[:, u % 2].bitcast(F32), op0=ALU.add,
                                                   op1=ALU.subtract).then_inc(q_split, 1)
                if stage == 4:
                    for t in tiles(u):
                        dve.wait_ge(mscore_ready, t + 1)
                        nc.vector.tensor_reduce(row_max[:, t], ps_h[t % 2][:].rearrange("p (h m) -> p h m", h=H),
                                                AX_X, ALU.max).then_inc(max_done, 1)
                if stage == 9:
                    dve.wait_ge(o_ready, 2 * (u + 1))
                    o = ps_o[:, 0:UT * NC * VW].rearrange("p (c w) -> p c w", w=VW)
                    r = rden[:, u].rearrange("p (c a) -> p c a", a=HC)
                    at = step(nc.vector.reciprocal(r, o[:, :, HC * HD:VW]))
                    dve.wait_ge(dve_step, at)
                    nc.vector.tensor_tensor(
                        attn[:, ts].rearrange("p j (c a d) -> p (j c) a d", c=NC, a=HC),
                        o[:, :, 0:HC * HD].rearrange("p c (a d) -> p c a d", a=HC),
                        r.unsqueeze(3).to_broadcast([P, UT * NC, HC, HD]), ALU.mult).then_inc(attn_ready, 1)
                if stage == 11:
                    dve.wait_ge(proj_ready, u + 1)
                    nc.vector.tensor_tensor(x1[:, ts].rearrange("p j d -> p (j d)"), ps_q[:, 0:UW],
                                            x_sb[:, ts].rearrange("p j d -> p (j d)"), ALU.add).then_inc(x1_ready, 1)
                    dve.wait_ge(x1_ready, u + 1)
                    normalise(U + u, lambda j: x1[:, u * UT + j], 1.0 + EPS, EPS * EPS)
                if stage == 12:
                    apply_norm(U + u)
                if stage == 13:
                    dve.wait_ge(t_hi_ready, u + 1)
                    nc.vector.scalar_tensor_tensor(out=t_lo[:, cols], in0=ps_t[:, 0:UW], scalar=pk2[:, SC0:SC0 + 1],
                                                   in1=t_hi[:, cols].bitcast(F32), op0=ALU.mult,
                                                   op1=ALU.subtract).then_inc(t_split, 1)
                if stage == 15:
                    choose(u)

            def weighted(s):
                width = group(STEPS[s][0])[1]
                dve.wait_ge(silu_done, s + 1)
                dve.wait_ge(row_in[s % NR], 16 * (s // NR + 1))
                if s - NW in SPLIT:
                    dve.wait_ge(z_split, SPLIT.index(s - NW) + 1)
                if s - NW in DIRECT:
                    dve.wait_ge(mlp2_done, s - NW + 1)
                nc.vector.scalar_tensor_tensor(out=z[:, s % NW, 0:width], in0=act_f[:, s % NF, 0:width], scalar=SILU_LIMIT,
                                               in1=row_all[:, s % NR, 0:width], op0=ALU.min,
                                               op1=ALU.mult).then_inc(z_ready, 1)

            def z_low(s):
                width = group(STEPS[s][0])[1]
                n = SPLIT.index(s)
                dve.wait_ge(z_hi_ready, n + 1)
                nc.vector.tensor_tensor(z_lo[:, n % NZ, 0:width], z[:, s % NW, 0:width],
                                        z_hi[:, n % NZ, 0:width].bitcast(F32), ALU.subtract).then_inc(z_split, 1)

            def residual(u):
                ts = slice(u * UT, (u + 1) * UT)
                dve.wait_ge(yt_ready, u + 1)
                dve.wait_ge(x1_ln_ready, u + 1)
                nc.vector.tensor_tensor(x_sb[:, ts].rearrange("p j d -> p (j d)"), ps_y[u % 2][:, 0:UW],
                                        x1_ln[:, ts].rearrange("p j d -> p (j d)"), ALU.add).then_inc(y_ready, 1)

            for kind, n in ORDER:
                if kind.startswith("stage"):
                    attention_stage(n, int(kind[5:]))
                if kind == "first_small":
                    small_operands()
                if kind == "keys":
                    key_block(n)
                if kind == "value_blocks":
                    value_blocks()
                if kind == "gate_small":
                    gate_and_biases()
                if kind == "route_weights":
                    route_weights(n)
                if kind == "weigh":
                    weighted(n)
                if kind == "low":
                    z_low(n)
                if kind == "out":
                    residual(n)


def kernel(**inputs):
    import concourse.bacc as bacc
    from concourse.bass_utils import run_bass_kernel_spmd

    def array(name):
        return np.asarray(inputs[name])

    def rows(a):
        return np.concatenate([a, np.zeros((P - a.shape[0], a.shape[1]), a.dtype)])

    first = np.concatenate(
        [array("ctx_1024").transpose(2, 0, 1).reshape(P, B * M), array("L0_xattn_Wk").T, array("L0_xattn_Wq").T]
        + [array(n).reshape(P, 1) for n in ("L0_xattn_bq", "L0_xattn_bk")], axis=1)
    second = np.concatenate(
        [array("L0_xattn_Wv").T, array("L0_xattn_Wo").T, array("L0_ffn_gate_w").T]
        + [array(n).reshape(P, 1) for n in ("L0_xattn_bv", "L0_ffn_scale")]
        + [rows(array("L0_ffn_gate_b").reshape(E, 1))]
        + [array("L0_ffn_mlp1_b").reshape(E, P, 2)[:, :, 0].T, rows(array("L0_ffn_mlp2_b"))], axis=1)
    arrays = {
        "x": array("x"),
        "first": first,
        "second": second,
        "w1": array("L0_ffn_mlp1_w").reshape(E, P, 2, P).transpose(2, 3, 0, 1).reshape(2, P, E * P),
        "w2": array("L0_ffn_mlp2_w").transpose(2, 0, 1).reshape(P, E * P),
    }
    nc = bacc.Bacc("TRN2", target_bir_lowering=False, num_devices=1)
    arrays = {f"{name}_dram": np.ascontiguousarray(a) for name, a in arrays.items()}
    handles = [nc.dram_tensor(name, a.shape, mybir.dt.from_np(a.dtype), kind="ExternalInput").ap()
               for name, a in arrays.items()]
    scratch = nc.dram_tensor("scratch_dram", (E, B * S), F32, kind="Internal").ap()
    out = nc.dram_tensor("out_dram", (B, S, P), F32, kind="ExternalOutput").ap()
    build_xattn_moe(nc, *handles, scratch, out)
    result = run_bass_kernel_spmd(nc, [arrays], core_ids=[0])
    return result.results[0]["out_dram"]
```
